# Optimizing a Trainium2 kernel written in Bass

```python
import numpy as np
import jax
import jax.numpy as jnp

def _softmax(x, axis=-1):
    return jax.nn.softmax(x, axis=axis)

def _gelu(x):
    return jax.nn.gelu(x, approximate=True)

def _silu(x):
    return jax.nn.silu(x)

def _sigmoid(x):
    return jax.nn.sigmoid(x)

def _layernorm(x, axis=-1, eps=1e-05):
    m = jnp.mean(x, axis=axis, keepdims=True)
    v = jnp.var(x, axis=axis, keepdims=True)
    return (x - m) / jnp.sqrt(v + eps)

def _scatter_add(tgt, idx, src, axis=0):
    return tgt.at[idx].add(src)

def _segment_sum(src, seg, n):
    return jax.ops.segment_sum(src, seg, n)
kernel_name = 'mk_adaln_ffn_d1_seqx_r4_560e10'

def setup_inputs(seed: int=0):
    np.random.seed(seed)
    _w = jnp.asarray

    def _rec_inputs():
        import jax
        import jax.numpy as jnp
        _rk = jax.random.key(seed)
        x = 0.5 + 0.2887 * jax.random.normal(jax.random.fold_in(_rk, 1), (16, 256, 256), jnp.float32)
        _lenS = 256 - jax.random.randint(jax.random.fold_in(_rk, 7), (16,), 0, max(1, 256 // 4) + 1, jnp.int32)
        _lenS2 = 256 - jax.random.randint(jax.random.fold_in(_rk, 8), (16,), 0, max(1, 256 // 4) + 1, jnp.int32)
        condB_zX = jax.random.uniform(jax.random.fold_in(_rk, 11), (16,), jnp.float32, 0.0, 0.983423)
        condB_zY = jax.random.uniform(jax.random.fold_in(_rk, 12), (16,), jnp.float32, 0.0, 0.979075)
        condB_zR = jax.random.uniform(jax.random.fold_in(_rk, 13), (16,), jnp.float32, 0.0, 0.9968)
        return (x, condB_zX, condB_zY, condB_zR)
    x, condB_zX, condB_zY, condB_zR = _rec_inputs()

    def _L0_cond_setup():
        import jax, jax.numpy as jnp
        import numpy as np
        key = jax.random.key(seed)
        k1, k2, k3, k4 = jax.random.split(key, 4)
        B, H, W = (64, 256, 256)
        return {'y': jax.random.uniform(k1, (B, H, W), dtype=jnp.float32), 'zX': jax.random.uniform(k2, (B, 1), dtype=jnp.float32), 'zY': jax.random.uniform(k3, (B, 1), dtype=jnp.float32), 'zR': jax.random.uniform(k4, (B, 1), dtype=jnp.float32), 'dx': 1, 'dy': 1}
    _L0_cond_all = _L0_cond_setup()
    _L0_cond_in = {k: v for k, v in _L0_cond_all.items() if k in ()}
    del _L0_cond_all

    def _L0_ffn_setup():
        import jax, jax.numpy as jnp
        import numpy as np
        S, B, H = (512, 1, 256)
        N_HEADS = 16
        HEAD_DIM = H // N_HEADS
        E, K, F = (8, 2, 512)
        EPS = 1e-05

        def layernorm(x, w, b):
            mu = jnp.mean(x, axis=-1, keepdims=True)
            var = jnp.mean(jnp.square(x - mu), axis=-1, keepdims=True)
            return (x - mu) * jax.lax.rsqrt(var + EPS) * w + b
        key = jax.random.key(seed)
        ks = jax.random.split(key, 8)
        std = 0.02
        return {'x': jax.random.normal(ks[0], (S, B, H), dtype=jnp.float32), 'ln1_w': jnp.ones((H,), jnp.float32), 'ln1_b': jnp.zeros((H,), jnp.float32), 'in_proj_w': jax.random.normal(ks[1], (3 * H, H), jnp.float32) * std, 'in_proj_b': jnp.zeros((3 * H,), jnp.float32), 'out_proj_w': jax.random.normal(ks[2], (H, H), jnp.float32) * std, 'out_proj_b': jnp.zeros((H,), jnp.float32), 'ln2_w': jnp.ones((H,), jnp.float32), 'ln2_b': jnp.zeros((H,), jnp.float32), 'router_w': jax.random.normal(ks[3], (E, H), jnp.float32) * std, 'w1': jax.random.normal(ks[4], (E, H, F), jnp.float32) * std, 'w2': jax.random.normal(ks[5], (E, F, H), jnp.float32) * std}
    _L0_ffn_all = _L0_ffn_setup()
    _L0_ffn_in = {k: v for k, v in _L0_ffn_all.items() if k in ('ln1_w', 'ln1_b', 'in_proj_w', 'in_proj_b', 'out_proj_w', 'out_proj_b', 'ln2_w', 'ln2_b', 'router_w', 'w1', 'w2')}
    del _L0_ffn_all
    return {'x': x, 'condB_zX': condB_zX, 'condB_zY': condB_zY, 'condB_zR': condB_zR, 'L0_ffn_ln1_w': _L0_ffn_in['ln1_w'], 'L0_ffn_ln1_b': _L0_ffn_in['ln1_b'], 'L0_ffn_in_proj_w': _L0_ffn_in['in_proj_w'], 'L0_ffn_in_proj_b': _L0_ffn_in['in_proj_b'], 'L0_ffn_out_proj_w': _L0_ffn_in['out_proj_w'], 'L0_ffn_out_proj_b': _L0_ffn_in['out_proj_b'], 'L0_ffn_ln2_w': _L0_ffn_in['ln2_w'], 'L0_ffn_ln2_b': _L0_ffn_in['ln2_b'], 'L0_ffn_router_w': _L0_ffn_in['router_w'], 'L0_ffn_w1': _L0_ffn_in['w1'], 'L0_ffn_w2': _L0_ffn_in['w2']}

def reference(x, condB_zX, condB_zY, condB_zR, L0_ffn_ln1_w, L0_ffn_ln1_b, L0_ffn_in_proj_w, L0_ffn_in_proj_b, L0_ffn_out_proj_w, L0_ffn_out_proj_b, L0_ffn_ln2_w, L0_ffn_ln2_b, L0_ffn_router_w, L0_ffn_w1, L0_ffn_w2):
    import jax
    import jax.numpy as jnp

    def _L0_cond_ref(y, zX, zY, zR, dx, dy):
        import jax, jax.numpy as jnp
        import numpy as np
        yp_x = jnp.pad(y, ((0, 0), (0, 0), (1, 1)), mode='reflect')
        lap_x = (yp_x[:, :, :-2] - 2.0 * y + yp_x[:, :, 2:]) / (dx * dx)
        yp_y = jnp.pad(y, ((0, 0), (1, 1), (0, 0)), mode='reflect')
        lap_y = (yp_y[:, :-2, :] - 2.0 * y + yp_y[:, 2:, :]) / (dy * dy)
        du_dt = zX[:, :, None] * lap_x + zY[:, :, None] * lap_y + zR[:, :, None] * y * (1.0 - y)
        return du_dt

    def _L0_ffn_ref(x, ln1_w, ln1_b, in_proj_w, in_proj_b, out_proj_w, out_proj_b, ln2_w, ln2_b, router_w, w1, w2):
        import jax, jax.numpy as jnp
        import numpy as np
        S, B, H = (512, 1, 256)
        N_HEADS = 16
        HEAD_DIM = H // N_HEADS
        E, K, F = (8, 2, 512)
        EPS = 1e-05

        def layernorm(x, w, b):
            mu = jnp.mean(x, axis=-1, keepdims=True)
            var = jnp.mean(jnp.square(x - mu), axis=-1, keepdims=True)
            return (x - mu) * jax.lax.rsqrt(var + EPS) * w + b
        s, b, h = x.shape
        hn = layernorm(x, ln1_w, ln1_b)
        qkv = hn @ in_proj_w.T + in_proj_b
        q, k, v = jnp.split(qkv, 3, axis=-1)
        q = q.reshape(s, b, N_HEADS, HEAD_DIM)
        k = k.reshape(s, b, N_HEADS, HEAD_DIM)
        v = v.reshape(s, b, N_HEADS, HEAD_DIM)
        scores = jnp.einsum('sbnd,tbnd->bnst', q, k) / np.sqrt(HEAD_DIM)
        causal = jnp.tril(jnp.ones((s, s), bool))
        scores = jnp.where(causal[None, None], scores, -jnp.inf)
        probs = jax.nn.softmax(scores, axis=-1)
        attn = jnp.einsum('bnst,tbnd->sbnd', probs, v).reshape(s, b, h)
        attn = attn @ out_proj_w.T + out_proj_b
        x1 = x + attn
        hn2 = layernorm(x1, ln2_w, ln2_b).reshape(s * b, h)
        logits = hn2 @ router_w.T
        rp = jax.nn.softmax(logits, axis=-1)
        topw, topi = jax.lax.top_k(rp, K)
        gates = jnp.sum(jax.nn.one_hot(topi, E, dtype=hn2.dtype) * topw[..., None], axis=1)
        hmid = jax.nn.gelu(jnp.einsum('th,ehf->tef', hn2, w1), approximate=False)
        y = jnp.einsum('tef,efh->th', hmid * gates[:, :, None], w2)
        return x1 + y.reshape(s, b, h)
    x = x + _L0_ffn_ref(_L0_cond_ref(x, condB_zX[:, None], condB_zY[:, None], condB_zR[:, None], 1, 1), L0_ffn_ln1_w, L0_ffn_ln1_b, L0_ffn_in_proj_w, L0_ffn_in_proj_b, L0_ffn_out_proj_w, L0_ffn_out_proj_b, L0_ffn_ln2_w, L0_ffn_ln2_b, L0_ffn_router_w, L0_ffn_w1, L0_ffn_w2)
    return x

_drawn_inputs = setup_inputs


def setup_inputs(seed=0):
    import zlib

    import numpy as np

    out = dict(_drawn_inputs(seed))
    spreads = {'L0_ffn_ln1_w': (1.0, 0.6),
     'L0_ffn_ln1_b': (0.0, 0.559),
     'L0_ffn_in_proj_b': (0.0, 0.1),
     'L0_ffn_out_proj_b': (0.0, 0.1),
     'L0_ffn_ln2_w': (1.0, 0.6),
     'L0_ffn_ln2_b': (0.0, 0.8)}
    factors = {}
    for name, (base, spread) in spreads.items():
        noise = np.random.default_rng([zlib.crc32(name.encode()), seed]).standard_normal(out[name].shape)
        drawn = base * np.exp(spread * noise) if base else spread * noise
        out[name] = jnp.asarray(drawn.astype(out[name].dtype))
    for name, factor in factors.items():
        out[name] = (out[name] * factor).astype(out[name].dtype)
    return out
```

```python
from contextlib import ExitStack

import concourse.bass as bass
from concourse import mybir

P = 128
F32 = mybir.dt.float32
F32R = mybir.dt.float32r
BF16 = mybir.dt.bfloat16
I32 = mybir.dt.int32
U32 = mybir.dt.uint32
ALU = mybir.AluOpType
ACT = mybir.ActivationFunctionType
AX = mybir.AxisListType.X
EPS = 1e-5


def adaln_moe_block(nc, x, zX, zY, zR, ln1_w, ln1_b, in_w, in_b, out_w, out_b, ln2_w, ln2_b,
                    router_w, w1, w2, out):
    S, B, H = x.shape
    NH, D = 16, H // 16
    E, _, F = w1.shape
    HC, FC = H // P, F // P
    CH = B // P
    G = CH * S
    TILES = 2 * S * B // P + E - 1
    ROWS = TILES * P
    SCALE = float(D) ** -0.5
    DU = 5
    TP = 4

    ctx = ExitStack()
    with ctx:
        def sb(name, shape, dt=F32):
            return ctx.enter_context(nc.sbuf_tensor(name, shape, dt))

        def psum(name, dt=F32):
            return ctx.enter_context(nc.psum_tensor(name, [P, 512], dt))

        def sem(name):
            return ctx.enter_context(nc.semaphore(name))

        hn2_d = nc.dram_tensor("hn2_d", [P, G, H], F32).ap()
        base_d = nc.dram_tensor("base_d", [P, G, H], F32).ap()
        xs_d = nc.dram_tensor("xs_d", [ROWS, H], F32).ap()
        ys_d = nc.dram_tensor("ys_d", [ROWS, H], F32).ap()

        ident = sb("ident", [P, P])
        ones_r = sb("ones_r", [2, P], F32R)
        lower = sb("lower", [P, P], BF16)
        ones_b = sb("ones_b", [P, P], BF16)
        ln = sb("ln", [P, 4, H])
        z = sb("z", [P, 3, S])
        alpha = sb("alpha", [P, S])
        wqkv_hi = sb("wqkv_hi", [P, HC, 3 * H], F32R)
        wqkv_lo = sb("wqkv_lo", [P, HC, 3 * H], F32R)
        wo_hi = sb("wo_hi", [P, HC, H], F32R)
        wo_lo = sb("wo_lo", [P, HC, H], F32R)
        bias = sb("bias", [2, 4 * H], F32R)
        wr = sb("wr", [P, HC, E])
        w1_hi = sb("w1_hi", [P, E * HC * F], F32R)
        w1_lo = sb("w1_lo", [P, E * HC * F], F32R)
        w2_s = sb("w2_s", [P, E * FC * H])
        kv = sb("kv", [P, 2 * S, H])
        xp = sb("xp", [P, 2, H + 2])
        xb = sb("xb", [P, 2, H])
        xud = sb("xud", [P, 2, 2, H])
        du = sb("du", [P, DU, H])
        mv = sb("mv", [P, 2, 2])
        rstd = sb("rstd", [P, 3])
        hn = sb("hn", [P, 2, 2, H])
        hT_hi = sb("hT_hi", [P, HC, P], F32R)
        hT_lo = sb("hT_lo", [P, HC, P], F32R)
        aT_hi = sb("aT_hi", [P, HC, P], F32R)
        aT_lo = sb("aT_lo", [P, HC, P], F32R)
        h2T = sb("h2T", [P, HC, P])
        q = sb("q", [P, 2, H])
        qk_prod = sb("qk_prod", [P, 2, TP * H])
        pv_prod = sb("pv_prod", [P, 3, TP * H])
        sc = sb("sc", [P, NH * S])
        pr = sb("pr", [P, NH * S])
        small = sb("small", [P, 96])
        x1 = sb("x1", [P, H])
        base = sb("base", [P, H])
        logits = sb("logits", [P, G, E])
        iota8 = sb("iota8", [P, E])
        iota_t = sb("iota_t", [P, TILES])
        iota_i = sb("iota_i", [P, TILES], I32)
        top8 = sb("top8", [P, G, 8])
        idx8 = sb("idx8", [P, G, 8], U32)
        idxf = sb("idxf", [P, G, 2])
        smalli = sb("smalli", [P, 8], I32)
        chosen = sb("chosen", [P, G * E], BF16)
        slot = sb("slot", [P, 2, G], U32)
        tab = sb("tab", [P, TILES], I32)
        xin = du[:, 0:2, :]
        xT_hi, xT_lo = hT_hi, hT_lo
        hm = xud[:, 0, :, :].rearrange("p a h -> p (a h)")
        hmT = qk_prod[:, :, 0:F]
        y = q

        b_tr = psum("b_tr")
        b_qk = psum("b_qk")
        b_v = psum("b_v")
        b_at = psum("b_at")
        b_x = psum("b_x")
        b_h = psum("b_h")
        b_t = psum("b_t")
        b_y = psum("b_y")

        names = """const_ready params_in win_in wT_ready wT_hi wT_lo wr_ready bias_in bias_split bias_lo_in
            w1_hi_ready w1_lo_ready w2_in zero_ready zero_done
            sums_ready scaled du_ready rstd1 rstd2 xhat1 xhat2 stats1 hn_ready hT_ready hT_hi_ready hT_lo_ready qkv_ready qkv_sb
            qk_used sc_ready exp_ready pv_piece pv_used at_ready aT_hi_ready aT_lo_ready o_ready x1_ready
            stats2 hn2_ready h2T_ready h2T_sb lg_ready lg_sb base_ready base_stored
            hn2_in rt_dve rt_exp rt_m rt_cum slots_ready scattered
            x_tr xT_hi_s xT_lo_s h_ready gelu_done hT2_ready hmT_sb y_ready y_sb
            out_ready dve_chain pool_chain act_chain alpha_ready""".split()
        s = {n: sem(n) for n in names}
        x_in = [sem(f"x_in{i}") for i in range(2)]
        xb_in = [sem(f"xb_in{i}") for i in range(2)]
        hn2_stored = [sem(f"hn2_stored{i}") for i in range(2)]
        halo_in = [sem(f"halo_in{i}") for i in range(2)]
        w1_staged = [sem(f"w1_staged{i}") for i in range(2)]
        xin_in = [sem(f"xin_in{i}") for i in range(2)]
        y_out = [sem(f"y_out{i}") for i in range(2)]
        g_in = [sem(f"g_in{i}") for i in range(2)]
        b_in = [sem(f"b_in{i}") for i in range(2)]
        o_out = [sem(f"o_out{i}") for i in range(2)]

        rt = pv_prod[:, 0, :].rearrange("p (a n) -> p a n", n=G * E)

        wT_parts = [part for k, (qk_bank, vo_bank) in enumerate(((b_tr, b_qk), (b_v, b_at))) for part in (
            (k, qk_bank, slice(0, 2 * H), wqkv_hi[:, k, 0:2 * H], wqkv_lo[:, k, 0:2 * H]),
            (k, vo_bank, slice(0, H), wqkv_hi[:, k, 2 * H:3 * H], wqkv_lo[:, k, 2 * H:3 * H]),
            (k, vo_bank, slice(H, 2 * H), wo_hi[:, k, :], wo_lo[:, k, :]))]

        wraw = kv[:, 0:8, :]
        w1raw = kv[:, 8:16, :]
        wrraw = kv[0:E, 16, :]
        braw = kv[0:1, 17:21, :]
        blo = w1_lo[0:1, (E - 1) * HC * F:E * HC * F]
        gath = pv_prod
        fin = qk_prod

        block = ctx.enter_context(nc.Block())

        def cg(g):
            return g // S, g % S

        NPIECE = [(g % S) // TP + 1 for g in range(G)]
        PIECES = [sum(NPIECE[:g]) for g in range(G + 1)]

        @block.sync
        def _(sp):
            for i, a in enumerate((ln1_w, ln1_b, ln2_w, ln2_b)):
                sp.dma_start(ln[:, i, :], a.rearrange("(o n) -> o n", o=1).to_broadcast([P, H])).then_inc(s["params_in"], 16)
            for i, a in enumerate((zX, zY, zR)):
                sp.dma_start(z[:, i, :], a.rearrange("(o n) -> o n", o=1).to_broadcast([P, S])).then_inc(s["params_in"], 16)
            sp.dma_start(wraw[:, 0:6, :], in_w.rearrange("(t p) h -> p t h", p=P)).then_inc(s["win_in"], 16)
            sp.dma_start(wraw[:, 6:8, :], out_w.rearrange("(t p) h -> p t h", p=P)).then_inc(s["win_in"], 16)
            sp.dma_start(wrraw, router_w).then_inc(s["win_in"], 16)
            sp.dma_start(braw[:, 0:3, :], in_b.rearrange("(o t h) -> o t h", o=1, h=H)).then_inc(s["win_in"], 16)
            sp.dma_start(braw[:, 3:4, :], out_b.rearrange("(o t h) -> o t h", o=1, h=H)).then_inc(s["win_in"], 16)

            def load(g):
                c, p = cg(g)
                i = g % 2
                if g >= 2:
                    sp.wait_ge(s["du_ready"], g - 1)
                sp.dma_start(xp[:, i, 1:H + 1], x[p, c * P:(c + 1) * P, :]).then_inc(x_in[i], 16)
                up, dn = xud[:, i, 0, :], xud[:, i, 1, :]
                if c == 0:
                    sp.dma_start(up[0:1, :], x[p, 1:2, :]).then_inc(x_in[i], 16)
                    sp.dma_start(up[1:P, :], x[p, 0:P - 1, :]).then_inc(x_in[i], 16)
                    sp.dma_start(dn, x[p, 1:P + 1, :]).then_inc(x_in[i], 16)
                else:
                    sp.dma_start(up, x[p, c * P - 1:(c + 1) * P - 1, :]).then_inc(x_in[i], 16)
                    sp.dma_start(dn[0:P - 1, :], x[p, c * P + 1:(c + 1) * P, :]).then_inc(x_in[i], 16)
                    sp.dma_start(dn[P - 1:P, :], x[p, B - 2:B - 1, :]).then_inc(x_in[i], 16)

            load(0)
            load(1)
            def stage_w1(e):
                if e >= 2:
                    sp.wait_ge(s["w1_lo_ready"], e - 1)
                sp.dma_start(w1raw[:, 4 * (e % 2):4 * (e % 2) + 4, :].rearrange("p (k u) h -> p k (u h)", k=HC),
                             w1[e].rearrange("(k p) f -> p k f", p=P)).then_inc(w1_staged[e % 2], 16)

            stage_w1(0)
            stage_w1(1)
            sp.dma_start(w2_s[:, :].rearrange("p (e k h) -> p e k h", e=E, k=FC),
                         w2.rearrange("e (k p) h -> p e k h", p=P)).then_inc(s["w2_in"], 16)
            sp.wait_ge(s["bias_split"], 2)
            sp.dma_start(bias[1:2, :].bitcast(F32), blo.bitcast(F32)).then_inc(s["bias_lo_in"], 16)
            sp.wait_ge(s["zero_ready"], 1)
            for t in range(0, TILES, 4):
                n = min(4, TILES - t)
                sp.dma_start(xs_d[t * P:(t + n) * P, :].rearrange("(t p) h -> p t h", p=P),
                             pv_prod[:, 2, 0:n * H].rearrange("p (t h) -> p t h", h=H)).then_inc(s["zero_done"], 16)
            for g in range(-3, G + 2):
                if 2 <= g + 4 < G:
                    load(g + 4)
                if 0 <= g < E - 2:
                    stage_w1(g + 2)
                if 0 <= g < G:
                    c, p = cg(g)
                    if g >= 2:
                        sp.wait_ge(s["base_ready"], g - 1)
                    sp.dma_start(xb[:, g % 2, :], x[p, c * P:(c + 1) * P, :]).then_inc(xb_in[g % 2], 16)
                if g - 2 >= 0:
                    sp.wait_ge(s["hn2_ready"], g - 1)
                    sp.dma_start(hn2_d[:, g - 2, :], hn[:, 1, g % 2, :]).then_inc(hn2_stored[g % 2], 16)
                if 0 <= g - 1 < G:
                    sp.wait_ge(s["base_ready"], g)
                    sp.dma_start(base_d[:, g - 1, :], base[:, :]).then_inc(s["base_stored"], 16)
            for i in range(2):
                sp.wait_ge(hn2_stored[i], 16 * (G // 2))
            sp.wait_ge(s["pv_piece"], PIECES[G])
            sp.dma_start(kv[:, :, :], hn2_d).then_inc(s["hn2_in"], 16)
            sp.wait_ge(s["scattered"], 16 * 2 * G)

            def tile_in(t, i):
                sp.dma_start(xin[:, i, :], xs_d[bass.ds(t * P, P), :]).then_inc(xin_in[i], 16)

            def tile_out(t, i):
                sp.dma_start(ys_d[bass.ds(t * P, P), :], y[:, i, :]).then_inc(y_out[i], 16)

            tile_in(0, 0)
            tile_in(1, 1)
            PAIRS = (TILES - 1) // 2
            with sp.Fori(0, PAIRS - 1) as n:
                for i in range(2):
                    sp.wait_ge(s["x_tr"], 2 * n + i + 1)
                    tile_in(2 * n + i + 2, i)
                    sp.wait_ge(s["y_sb"], 2 * n + i + 1)
                    tile_out(2 * n + i, i)
            for t in range(2 * PAIRS - 2, TILES):
                if t + 2 < TILES:
                    sp.wait_ge(s["x_tr"], t + 1)
                    tile_in(t + 2, t % 2)
                sp.wait_ge(s["y_sb"], t + 1)
                tile_out(t, t % 2)
            for g in range(G):
                c, p = cg(g)
                if g == 0:
                    sp.wait_ge(s["base_stored"], 16 * G)
                if g >= 2:
                    sp.wait_ge(s["out_ready"], g - 1)
                sp.dma_start(xp[:, g % 2, 0:H], base_d[:, g, :]).then_inc(b_in[g % 2], 16)
                if g >= 1:
                    cc, pp = cg(g - 1)
                    sp.wait_ge(s["out_ready"], g)
                    sp.dma_start(out[pp, cc * P:(cc + 1) * P, :], fin[:, (g - 1) % 2, 0:H]).then_inc(o_out[(g - 1) % 2], 16)
            cc, pp = cg(G - 1)
            sp.wait_ge(s["out_ready"], G)
            sp.dma_start(out[pp, cc * P:(cc + 1) * P, :], fin[:, (G - 1) % 2, 0:H]).then_inc(o_out[(G - 1) % 2], 16)
            sp.wait_ge(o_out[0], 16 * (G // 2))
            sp.wait_ge(o_out[1], 16 * (G // 2))

        @block.gpsimd
        def _(pool):
            n = [0]

            def link(ins):
                n[0] += 1
                ins.then_inc(s["pool_chain"], 1)
                pool.wait_ge(s["pool_chain"], n[0])

            link(pool.memset(rstd[:, 2:3], -0.5))
            link(pool.memset(ident[:, :], 0.0))
            pool.affine_select(out=ident[:, :], in_=ident[:, :], compare_op=ALU.not_equal, fill=1.0, base=0,
                               pattern=[[-1, P]], channel_multiplier=1).then_inc(s["const_ready"], 1)
            link(pool.memset(ones_b[:, :], 1.0))
            pool.affine_select(out=lower[:, :], in_=ones_b[:, :], compare_op=ALU.is_gt, fill=0.0, base=0,
                               pattern=[[1, P]], channel_multiplier=-1).then_inc(s["const_ready"], 1)
            pool.memset(ones_r[:, :].bitcast(F32), 1.0).then_inc(s["const_ready"], 1)
            pool.memset(pv_prod[:, 2, :], 0.0).then_inc(s["zero_ready"], 1)
            link(pool.iota(iota_i[:, :], [[1, TILES]], base=0, channel_multiplier=0))
            link(pool.tensor_copy(iota_t[:, :], iota_i[:, :]))
            pool.tensor_copy(iota8[:, :], iota_i[:, 0:E]).then_inc(s["const_ready"], 1)
            pool.wait_ge(s["params_in"], 16 * 7)
            link(pool.tensor_tensor(alpha[:, :], z[:, 0, :], z[:, 1, :], ALU.add))
            link(pool.tensor_scalar(alpha[:, :], alpha[:, :], -2.0, None, ALU.mult))
            link(pool.tensor_tensor(alpha[:, :], alpha[:, :], z[:, 2, :], ALU.add))
            pool.tensor_scalar(small[:, 80:80 + S], z[:, 2, :], -1.0, None, ALU.mult).then_inc(s["alpha_ready"], 1)

            def w1_low(e):
                pool.wait_ge(s["w1_hi_ready"], e + 1)
                part = slice(e * HC * F, (e + 1) * HC * F)
                pool.tensor_tensor(w1_lo[:, part], w1raw[:, 4 * (e % 2):4 * (e % 2) + 4, :].rearrange("p a h -> p (a h)"),
                                   w1_hi[:, part].bitcast(F32), ALU.subtract).then_inc(s["w1_lo_ready"], 1)

            def neighbours(g):
                i = g % 2
                pool.wait_ge(x_in[i], 64 * (g // 2 + 1))
                link(pool.tensor_copy(xp[:, i, 0:H + 2:H + 1], xp[:, i, 2:H:H - 3]))
                link(pool.tensor_tensor(xud[:, i, 0, :], xud[:, i, 0, :], xud[:, i, 1, :], ALU.add))
                pool.tensor_tensor(xud[:, i, 1, :], xp[:, i, 0:H], xp[:, i, 2:H + 2], ALU.add).then_inc(s["sums_ready"], 1)

            def diffuse(g):
                i = g % 2
                d = du[:, g % DU, :]
                pool.wait_ge(s["scaled"], 3 * (g + 1))
                link(pool.tensor_tensor(d, d, xp[:, i, 1:H + 1], ALU.mult))
                link(pool.tensor_tensor(d, d, xud[:, i, 0, :], ALU.add))
                pool.tensor_tensor(d, d, xud[:, i, 1, :], ALU.add).then_inc(s["du_ready"], 1)

            def deviation(g, k):
                pool.wait_ge(s[("stats1", "stats2")[k]], g + 1)
                link(pool.tensor_scalar(rstd[:, k:k + 1], mv[:, k, 1:2], EPS, None, ALU.add))
                pool.tensor_tensor(rstd[:, k:k + 1], rstd[:, k:k + 1], rstd[:, 2:3], ALU.pow).then_inc(s[("rstd1", "rstd2")[k]], 1)

            def affine(g, k):
                row = hn[:, k, g % 2, :]
                pool.wait_ge(s[("xhat1", "xhat2")[k]], g + 1)
                link(pool.tensor_tensor(row, row, ln[:, 2 * k, :], ALU.mult))
                pool.tensor_tensor(row, row, ln[:, 2 * k + 1, :], ALU.add).then_inc(s[("hn_ready", "hn2_ready")[k]], 1)

            for g in range(-3, G + 2):
                if 0 <= g + 2 < G:
                    deviation(g + 2, 0)
                if 0 <= g - 2:
                    affine(g - 2, 1)
                if g + 3 < G:
                    neighbours(g + 3)
                    diffuse(g + 3)
                if 0 <= g - 1 < G:
                    deviation(g - 1, 1)
                if 0 <= g + 2 < G:
                    affine(g + 2, 0)
                if 0 <= g - 1 < G:
                    pool.wait_ge(xb_in[(g - 1) % 2], 16 * ((g - 1) // 2 + 1))
                    pool.wait_ge(s["x1_ready"], g)
                    if g - 1 >= 1:
                        pool.wait_ge(s["base_stored"], 16 * (g - 1))
                    pool.tensor_tensor(base[:, :], x1[:, :], xb[:, (g - 1) % 2, :], ALU.add).then_inc(s["base_ready"], 1)
                if 0 <= g < E:
                    if g == E - 1:
                        pool.wait_ge(s["bias_lo_in"], 16)
                    w1_low(g)
            pool.wait_ge(s["slots_ready"], 1)
            pool.wait_ge(s["hn2_in"], 16)
            pool.wait_ge(s["zero_done"], 16 * ((TILES + 3) // 4))
            for g in range(G):
                for k in range(2):
                    pool.indirect_dma_start(xs_d, bass.IndirectOffsetOnAxis(ap=slot[:, k, g:g + 1], axis=0),
                                            kv[:, g, :], None).then_inc(s["scattered"], 16)
            pool.wait_ge(y_out[0], 16 * ((TILES + 1) // 2))
            pool.wait_ge(y_out[1], 16 * (TILES // 2))
            for g in range(G):
                if g >= 2:
                    pool.wait_ge(s["out_ready"], g - 1)
                for k in range(2):
                    pool.indirect_dma_start(gath[:, g % 2, k * H:(k + 1) * H], None, ys_d,
                                            bass.IndirectOffsetOnAxis(ap=slot[:, k, g:g + 1], axis=0)).then_inc(g_in[g % 2], 16)

        @block.scalar
        def _(act):
            def w1_high(e):
                act.wait_ge(w1_staged[e % 2], 16 * (e // 2 + 1))
                part = slice(e * HC * F, (e + 1) * HC * F)
                act.activation(w1_hi[:, part], w1raw[:, 4 * (e % 2):4 * (e % 2) + 4, :].rearrange("p a h -> p (a h)"),
                               ACT.Copy).then_inc(s["w1_hi_ready"], 1)

            for n, (_, bank, cols, hi, _) in enumerate(wT_parts):
                act.wait_ge(s["wT_ready"], n // 3 * 2 + (1 if n % 3 == 0 else 2))
                act.activation(hi, bank[:, cols], ACT.Copy).then_inc(s["wT_hi"], 1)
            act.wait_ge(s["wT_ready"], 5)
            act.activation(wr[:, :, :].rearrange("p k e -> p (k e)"), b_x[:, 0:HC * E], ACT.Copy).then_inc(s["wr_ready"], 1)
            act.activation(bias[0:1, :], braw.rearrange("o a h -> o (a h)"), ACT.Copy).then_inc(s["bias_split"], 1)

            def scale(g):
                i, p = g % 2, g % S
                if g == 0:
                    act.wait_ge(s["alpha_ready"], 1)
                if g >= DU:
                    act.wait_ge(s["x1_ready"], g - DU + 1)
                act.wait_ge(x_in[i], 64 * (g // 2 + 1))
                act.activation(du[:, g % DU, :], xp[:, i, 1:H + 1], ACT.Identity, bias=alpha[:, p:p + 1],
                               scale=small[:, 80 + p:81 + p]).then_inc(s["scaled"], 1)
                act.wait_ge(s["sums_ready"], g + 1)
                act.activation(xud[:, i, 0, :], xud[:, i, 0, :], ACT.Copy, scale=z[:, 1, p:p + 1]).then_inc(s["scaled"], 1)
                act.activation(xud[:, i, 1, :], xud[:, i, 1, :], ACT.Copy, scale=z[:, 0, p:p + 1]).then_inc(s["scaled"], 1)

            for g in range(-3, G + 2):
                if 0 <= g - 1 < G:
                    act.wait_ge(s["pv_used"], PIECES[g])
                    if g - 1 >= 1:
                        act.wait_ge(s["o_ready"], g - 1)
                    act.activation(aT_hi[:, :, :].rearrange("p k b -> p (k b)"), b_at[:, 0:H], ACT.Copy).then_inc(s["aT_hi_ready"], 1)
                if 0 <= g + 1 < G:
                    act.wait_ge(s["hT_ready"], g + 2)
                    if g + 1 >= 1:
                        act.wait_ge(s["qkv_ready"], g + 1)
                    act.activation(hT_hi[:, :, :].rearrange("p k b -> p (k b)"), b_tr[:, 0:H], ACT.Copy).then_inc(s["hT_hi_ready"], 1)
                if g + 3 < G:
                    scale(g + 3)
                if 0 <= g + 1 < E:
                    w1_high(g + 1)
                if 0 <= g < G:
                    n = NH * (g % S + 1)
                    act.wait_ge(s["sc_ready"], g + 1)
                    act.activation(pr[:, 0:n], sc[:, 0:n], ACT.Exp, scale=SCALE).then_inc(s["exp_ready"], 1)
                if 0 <= g + 1 < G:
                    p = (g + 1) % S
                    act.wait_ge(s["qkv_ready"], g + 2)
                    act.activation(q[:, (g + 1) % 2, :], b_qk[:, 0:H], ACT.Copy).then_inc(s["qkv_sb"], 1)
                    if p == 8:
                        act.wait_ge(s["w1_lo_ready"], E)
                    act.activation(kv[:, p, :], b_qk[:, H:2 * H], ACT.Copy).then_inc(s["qkv_sb"], 1)
                    if p == 0 and g >= 0:
                        act.wait_ge(s["pv_piece"], PIECES[g + 1])
                    act.activation(kv[:, S + p, :], b_v[:, 0:H], ACT.Copy).then_inc(s["qkv_sb"], 1)
                if g - 2 >= 0:
                    act.wait_ge(s["h2T_ready"], g - 1)
                    if g - 2 >= 1:
                        act.wait_ge(s["lg_ready"], g - 2)
                    act.activation(h2T[:, :, :].rearrange("p k b -> p (k b)"), b_tr[:, 0:H], ACT.Copy).then_inc(s["h2T_sb"], 1)
                    act.wait_ge(s["lg_ready"], g - 1)
                    act.activation(logits[:, g - 2, :], b_tr[:, H:H + E], ACT.Copy).then_inc(s["lg_sb"], 1)
            act.wait_ge(s["rt_dve"], 1)
            act.activation(rt[:, 0, :], rt[:, 0, :], ACT.Exp).then_inc(s["rt_exp"], 1)

            def split(t):
                act.wait_ge(s["x_tr"], t + 1)
                act.activation(xT_hi[:, :, :].rearrange("p k b -> p (k b)"), b_x[:, 0:H], ACT.Copy).then_inc(s["xT_hi_s"], 1)

            def gelu(t):
                act.wait_ge(s["h_ready"], t + 1)
                act.activation(hm[:, :], b_h[:, :], ACT.Gelu).then_inc(s["gelu_done"], 1)

            def turned(t, i):
                act.wait_ge(s["hT2_ready"], t + 1)
                act.activation(hmT[:, i, :], b_t[:, :], ACT.Copy).then_inc(s["hmT_sb"], 1)

            split(0)
            gelu(0)
            with act.Fori(0, (TILES - 1) // 2) as n:
                for i in range(2):
                    t = 2 * n + 1 + i
                    act.wait_ge(s["h_ready"], t)
                    split(t)
                    turned(t - 1, i)
                    gelu(t)
            turned(TILES - 1, (TILES - 1) % 2)

        @block.vector
        def _(dve):
            cnt = [0]

            def link(ins):
                cnt[0] += 1
                ins.then_inc(s["dve_chain"], 1)
                dve.wait_ge(s["dve_chain"], cnt[0])

            for n, (_, bank, cols, hi, lo) in enumerate(wT_parts):
                dve.wait_ge(s["wT_hi"], 3 * (n // 3) + 3)
                dve.tensor_tensor(lo, bank[:, cols], hi.bitcast(F32), ALU.subtract).then_inc(s["wT_lo"], 1)
            dve.wait_ge(s["bias_split"], 1)
            dve.tensor_tensor(blo, braw.rearrange("o a h -> o (a h)"), bias[0:1, :].bitcast(F32), ALU.subtract).then_inc(s["bias_split"], 1)

            def stats(src, g, k):
                link(dve.bn_stats(small[:, 48:54], src))
                dve.bn_aggr(mv[:, k, :], small[:, 48:54]).then_inc(s[("stats1", "stats2")[k]], 1)

            def unit(src, g, k):
                dve.wait_ge(s[("rstd1", "rstd2")[k]], g + 1)
                if g >= 2:
                    dve.wait_ge(s[("hT_ready", "h2T_ready")[k]], g - 1)
                    if k == 1:
                        dve.wait_ge(hn2_stored[g % 2], 16 * (g // 2))
                dve.tensor_scalar(hn[:, k, g % 2, :], src, mv[:, k, 0:1], rstd[:, k:k + 1], ALU.subtract,
                                  ALU.mult).then_inc(s[("xhat1", "xhat2")[k]], 1)

            piece = [0]
            for g in range(-3, G + 2):
                T = g % S + 1
                if 0 <= g + 2 < G:
                    dve.wait_ge(s["du_ready"], g + 3)
                    if g + 2 >= 1:
                        dve.wait_ge(s["xhat1"], g + 2)
                    stats(du[:, (g + 2) % DU, :], g + 2, 0)
                if 0 <= g - 1 < G:
                    dve.wait_ge(s["aT_hi_ready"], g)
                    dve.tensor_tensor(aT_lo[:, :, :].rearrange("p k b -> p (k b)"), b_at[:, 0:H],
                                      aT_hi[:, :, :].rearrange("p k b -> p (k b)").bitcast(F32), ALU.subtract).then_inc(s["aT_lo_ready"], 1)
                if 0 <= g < G:
                    dve.wait_ge(s["qkv_sb"], 3 * (g + 1))
                    for m, t0 in enumerate(range(0, T, TP)):
                        t1 = min(T, t0 + TP)
                        prod = qk_prod[:, m % 2, 0:(t1 - t0) * H]
                        link(dve.tensor_tensor(prod.rearrange("p (t h) -> p t h", h=H),
                                               q[:, g % 2, :].rearrange("p (o h) -> p o h", o=1).to_broadcast([P, t1 - t0, H]),
                                               kv[:, t0:t1, :], ALU.mult))
                        link(dve.tensor_reduce(sc[:, 0:NH * T].rearrange("p (n t) -> p t n", t=T)[:, t0:t1, :],
                                               prod.rearrange("p (t n d) -> p t n d", n=NH, d=D), AX, ALU.add))
                if 0 <= g + 1 < G:
                    dve.wait_ge(s["hT_hi_ready"], g + 2)
                    dve.tensor_tensor(hT_lo[:, :, :].rearrange("p k b -> p (k b)"), b_tr[:, 0:H],
                                      hT_hi[:, :, :].rearrange("p k b -> p (k b)").bitcast(F32), ALU.subtract).then_inc(s["hT_lo_ready"], 1)
                if 0 <= g < G:
                    scv = sc[:, 0:NH * T].rearrange("p (n t) -> p n t", t=T)
                    link(dve.tensor_reduce(small[:, 0:NH], scv, AX, ALU.max))
                    dve.tensor_tensor(scv, scv, small[:, 0:NH].rearrange("p (n o) -> p n o", o=1).to_broadcast([P, NH, T]),
                                      ALU.subtract).then_inc(s["sc_ready"], 1)
                if 0 <= g - 1 < G:
                    dve.wait_ge(s["o_ready"], g)
                    if g - 1 >= 1:
                        dve.wait_ge(s["base_ready"], g - 1)
                    dve.tensor_tensor(x1[:, :], du[:, (g - 1) % DU, :], b_at[:, H:2 * H], ALU.add).then_inc(s["x1_ready"], 1)
                    dve.wait_ge(s["x1_ready"], g)
                    if g - 1 >= 1:
                        dve.wait_ge(s["xhat2"], g - 1)
                    stats(x1[:, :], g - 1, 1)
                if 0 <= g + 2 < G:
                    unit(du[:, (g + 2) % DU, :], g + 2, 0)
                if 0 <= g < G:
                    dve.wait_ge(s["exp_ready"], g + 1)
                    prv = pr[:, 0:NH * T].rearrange("p (n t) -> p n t", t=T)
                    link(dve.tensor_reduce(small[:, 16:16 + NH], prv, AX, ALU.add))
                    link(dve.reciprocal(small[:, 32:32 + NH], small[:, 16:16 + NH]))
                    link(dve.tensor_tensor(prv, prv, small[:, 32:32 + NH].rearrange("p (n o) -> p n o", o=1).to_broadcast([P, NH, T]), ALU.mult))
                    for t0 in range(0, T, TP):
                        t1 = min(T, t0 + TP)
                        r = piece[0] % 3
                        if piece[0] >= 3:
                            dve.wait_ge(s["pv_used"], piece[0] - 2)
                        elif r == 2:
                            dve.wait_ge(s["zero_done"], 16 * ((TILES + 3) // 4))
                        dve.tensor_tensor(pv_prod[:, r, 0:(t1 - t0) * H].rearrange("p (t n d) -> p t n d", n=NH, d=D),
                                          kv[:, S + t0:S + t1, :].rearrange("p t (n d) -> p t n d", d=D),
                                          pr[:, 0:NH * T].rearrange("p (n t o) -> p t n o", t=T, o=1)[:, t0:t1, :, :].to_broadcast([P, t1 - t0, NH, D]),
                                          ALU.mult).then_inc(s["pv_piece"], 1)
                        piece[0] += 1
                if 0 <= g - 1 < G:
                    unit(x1[:, :], g - 1, 1)

            dve.wait_ge(s["lg_sb"], G)
            dve.wait_ge(s["const_ready"], 4)
            A = rt[:, 0, :].rearrange("p (g e) -> p g e", e=E)
            Bv = rt[:, 1, :].rearrange("p (g e) -> p g e", e=E)
            Cv = rt[:, 2, :].rearrange("p (g e) -> p g e", e=E)
            col = rt[:, 3, 0:G]
            colb = col.rearrange("p (g o) -> p g o", o=1).to_broadcast([P, G, E])
            link(dve.tensor_reduce(col, logits[:, :, :], AX, ALU.max))
            dve.tensor_tensor(A, logits[:, :, :], colb, ALU.subtract).then_inc(s["rt_dve"], 1)
            dve.wait_ge(s["rt_exp"], 1)
            link(dve.tensor_reduce(col, A, AX, ALU.add))
            link(dve.reciprocal(col, col))
            link(dve.tensor_tensor(A, A, colb, ALU.mult))
            for g in range(G):
                link(dve.max(top8[:, g, :], A[:, g, :]))
                link(dve.max_index(idx8[:, g, :], top8[:, g, :], A[:, g, :]))
            link(dve.tensor_copy(idxf[:, :, :], idx8[:, :, 0:2]))
            io = iota8[:, :].rearrange("p (o e) -> p o e", o=1).to_broadcast([P, G, E])
            for k, oh in ((0, A), (1, Bv)):
                link(dve.tensor_tensor(oh, io, idxf[:, :, k:k + 1].to_broadcast([P, G, E]), ALU.is_equal))
            dve.tensor_tensor(chosen[:, :].rearrange("p (g e) -> p g e", e=E), A, Bv, ALU.add).then_inc(s["rt_m"], 1)
            dve.wait_ge(s["rt_cum"], 1)
            cum = b_tr[:, 0:G * E].rearrange("p (g e) -> p g e", e=E)
            tot = b_tr[:, G * E:2 * G * E].rearrange("p (g e) -> p g e", e=E)
            D0 = rt[:, 3, :].rearrange("p (g e) -> p g e", e=E)
            link(dve.tensor_copy(Cv, tot))
            src, dst, step = Cv, D0, 1
            while step < G:
                link(dve.tensor_copy(dst[:, 0:step, :], src[:, 0:step, :]))
                link(dve.tensor_tensor(dst[:, step:G, :], src[:, step:G, :], src[:, 0:G - step, :], ALU.add))
                src, dst, step = dst, src, 2 * step
            incl, spare = src, dst
            cntf, nt, endt, nti, bs = (small[:, 0:8], small[:, 8:16], small[:, 16:24], smalli[:, 0:8], small[:, 24:32])
            link(dve.tensor_scalar(nti, incl[:, G - 1, :], float(P - 1), None, ALU.add))
            link(dve.tensor_scalar(nti, nti, 7, None, ALU.arith_shift_right))
            link(dve.tensor_copy(nt, nti))
            link(dve.memset(cntf, 1.0))
            link(dve.tensor_tensor_scan(endt, cntf, nt, 0.0, ALU.mult, ALU.add))
            link(dve.tensor_tensor(bs, endt, nt, ALU.subtract))
            link(dve.tensor_scalar(bs, bs, float(P), None, ALU.mult))
            link(dve.tensor_tensor(spare, incl, tot, ALU.subtract))
            link(dve.tensor_tensor(spare, spare, cum, ALU.add))
            link(dve.tensor_tensor(spare, spare, bs.rearrange("p (o e) -> p o e", o=1).to_broadcast([P, G, E]), ALU.add))
            for k, oh in ((0, A), (1, Bv)):
                link(dve.tensor_tensor(oh, oh, spare, ALU.mult))
                link(dve.tensor_reduce(idxf[:, :, 0], oh, AX, ALU.add))
                link(dve.tensor_copy(slot[:, k, :], idxf[:, :, 0]))
            dve.engine_nop().then_inc(s["slots_ready"], 1) if False else None
            tt = qk_prod[:, 0, 0:TILES * E].rearrange("p (t e) -> p t e", e=E)
            link(dve.tensor_tensor(tt, iota_t[:, :].rearrange("p (t o) -> p t o", o=1).to_broadcast([P, TILES, E]),
                                   endt.rearrange("p (o e) -> p o e", o=1).to_broadcast([P, TILES, E]), ALU.is_ge))
            link(dve.tensor_reduce(qk_prod[:, 1, 0:TILES], tt, AX, ALU.add))
            link(dve.tensor_scalar(qk_prod[:, 1, 0:TILES], qk_prod[:, 1, 0:TILES], float(E - 1), None, ALU.min))
            dve.tensor_copy(tab[:, :], qk_prod[:, 1, 0:TILES]).then_inc(s["slots_ready"], 1)

            def low(t):
                dve.wait_ge(s["xT_hi_s"], t + 1)
                dve.tensor_tensor(xT_lo[:, :, :].rearrange("p k b -> p (k b)"), b_x[:, 0:H],
                                  xT_hi[:, :, :].rearrange("p k b -> p (k b)").bitcast(F32), ALU.subtract).then_inc(s["xT_lo_s"], 1)

            def result(t, i, first):
                dve.wait_ge(s["y_ready"], t + 1)
                if not first:
                    dve.wait_ge(y_out[i], 16 * y_before(t, i))
                dve.tensor_copy(y[:, i, :], b_y[:, 0:H]).then_inc(s["y_sb"], 1)

            def y_before(t, i):
                return (t - i) // 2 if isinstance(t, int) else None

            low(0)
            low(1)
            result(0, 0, True)
            low(2)
            result(1, 1, True)
            with dve.Fori(0, (TILES - 3) // 2) as n:
                for i in range(2):
                    low(2 * n + 3 + i)
                    dve.wait_ge(s["y_ready"], 2 * n + 3 + i)
                    dve.wait_ge(y_out[i], 16 * n + 16)
                    dve.tensor_copy(y[:, i, :], b_y[:, 0:H]).then_inc(s["y_sb"], 1)
            result(TILES - 1, (TILES - 1) % 2, False)
            for g in range(G):
                dve.wait_ge(b_in[g % 2], 16 * (g // 2 + 1))
                dve.wait_ge(g_in[g % 2], 32 * (g // 2 + 1))
                if g >= 2:
                    dve.wait_ge(o_out[g % 2], 16 * (g // 2))
                link(dve.scalar_tensor_tensor(out=xp[:, g % 2, 0:H], in0=gath[:, g % 2, 0:H], scalar=top8[:, g, 0:1],
                                              in1=xp[:, g % 2, 0:H], op0=ALU.mult, op1=ALU.add))
                dve.scalar_tensor_tensor(out=fin[:, g % 2, 0:H], in0=gath[:, g % 2, H:2 * H], scalar=top8[:, g, 1:2],
                                         in1=xp[:, g % 2, 0:H], op0=ALU.mult, op1=ALU.add).then_inc(s["out_ready"], 1)

        @block.tensor
        def _(pe):
            pe.wait_ge(s["const_ready"], 4)
            pe.wait_ge(s["win_in"], 16 * 5)
            for k in range(HC):
                for t in range(4):
                    mm = pe.transpose((b_tr, b_v)[k][:, t * P:(t + 1) * P], wraw[:, t, k * P:(k + 1) * P], ident[:, :])
                mm.then_inc(s["wT_ready"], 1)
                for t in range(4):
                    mm = pe.transpose((b_qk, b_at)[k][:, t * P:(t + 1) * P], wraw[:, 4 + t, k * P:(k + 1) * P], ident[:, :])
                mm.then_inc(s["wT_ready"], 1)
            for k in range(HC):
                mm = pe.transpose(b_x[:, k * E:(k + 1) * E], wrraw[:, k * P:(k + 1) * P], ident[0:E, 0:E])
            mm.then_inc(s["wT_ready"], 1)

            def three(dst, hi, lo, w_hi, w_lo, rows, start):
                for k in range(HC):
                    pe.matmul(dst, hi[:, k, :], w_hi(k), start=(start and k == 0), stop=False)
                    pe.matmul(dst, hi[:, k, :], w_lo(k), start=False, stop=False)
                    mm = pe.matmul(dst, lo[:, k, :], w_hi(k), start=False, stop=(k == HC - 1))
                return mm

            piece = [0]
            for g in range(-1, G + 2):
                if g + 1 < G:
                    pe.wait_ge(s["hn_ready"], g + 2)
                    if g == -1:
                        pe.wait_ge(s["wT_lo"], 6)
                        pe.wait_ge(s["wr_ready"], 1)
                        pe.wait_ge(s["bias_lo_in"], 16)
                    if g - 3 >= 0:
                        pe.wait_ge(s["lg_sb"], g - 2)
                    for k in range(HC):
                        mm = pe.transpose(b_tr[:, k * P:(k + 1) * P], hn[:, 0, (g + 1) % 2, k * P:(k + 1) * P], ident[:, :])
                    mm.then_inc(s["hT_ready"], 1)
                if 0 <= g - 1 < G:
                    pe.wait_ge(s["aT_lo_ready"], g)
                    pe.matmul(b_at[:, H:2 * H], ones_r[:, :], bias[:, 3 * H:4 * H], start=True, stop=False)
                    three(b_at[:, H:2 * H], aT_hi, aT_lo, lambda k: wo_hi[:, k, :], lambda k: wo_lo[:, k, :], None,
                          False).then_inc(s["o_ready"], 1)
                if g + 1 < G:
                    pe.wait_ge(s["hT_lo_ready"], g + 2)
                    pe.wait_ge(s["qkv_sb"], 3 * (g + 1))
                    for bank, a, b in ((b_qk, 0, 2 * H), (b_v, 2 * H, 3 * H)):
                        pe.matmul(bank[:, 0:b - a], ones_r[:, :], bias[:, a:b], start=True, stop=False)
                        mm = three(bank[:, 0:b - a], hT_hi, hT_lo, lambda k: wqkv_hi[:, k, a:b],
                                   lambda k: wqkv_lo[:, k, a:b], None, False)
                    mm.then_inc(s["qkv_ready"], 1)
                if g - 2 >= 0:
                    pe.wait_ge(s["hn2_ready"], g - 1)
                    if g - 3 >= 0:
                        pe.wait_ge(s["lg_sb"], g - 2)
                    for k in range(HC):
                        mm = pe.transpose(b_tr[:, k * P:(k + 1) * P], hn[:, 1, g % 2, k * P:(k + 1) * P], ident[:, :])
                    mm.then_inc(s["h2T_ready"], 1)
                if 0 <= g < G:
                    T = g % S + 1
                    if g >= 1:
                        pe.wait_ge(s["x1_ready"], g)
                    for t0 in range(0, T, TP):
                        t1 = min(T, t0 + TP)
                        r = piece[0] % 3
                        pe.wait_ge(s["pv_piece"], piece[0] + 1)
                        for t in range(t0, t1):
                            for k in range(HC):
                                mm = pe.matmul(b_at[:, k * P:(k + 1) * P], pv_prod[:, r, (t - t0) * H + k * P:(t - t0) * H + (k + 1) * P],
                                               ident[:, :], start=(t == 0 and k == 0), stop=(t == T - 1),
                                               skip_group_check=True)
                        mm.then_inc(s["pv_used"], 1)
                        piece[0] += 1
                if g - 2 >= 0:
                    pe.wait_ge(s["h2T_sb"], g - 1)
                    for k in range(HC):
                        mm = pe.matmul(b_tr[:, H:H + E], h2T[:, k, :], wr[:, k, :], start=(k == 0), stop=(k == HC - 1))
                    mm.then_inc(s["lg_ready"], 1)
            pe.wait_ge(s["rt_m"], 1)
            pe.matmul(b_tr[:, 0:G * E], lower[:, :], chosen[:, :], start=True, stop=True)
            pe.matmul(b_tr[:, G * E:2 * G * E], ones_b[:, :], chosen[:, :], start=True, stop=True).then_inc(s["rt_cum"], 1)
            pe.wait_ge(s["slots_ready"], 1)

            def turn_in(t, i, count):
                pe.wait_ge(xin_in[i], count)
                pe.wait_ge(s["xT_lo_s"], t) if not (isinstance(t, int) and t == 0) else None
                for k in range(HC):
                    mm = pe.transpose(b_x[:, k * P:(k + 1) * P], xin[:, i, k * P:(k + 1) * P], ident[:, :])
                mm.then_inc(s["x_tr"], 1)

            def up(t):
                e = pe.value_load(tab[0:1, bass.ds(t, 1)], min_val=0, max_val=E - 1)
                pe.wait_ge(s["xT_lo_s"], t + 1)
                if not (isinstance(t, int) and t == 0):
                    pe.wait_ge(s["gelu_done"], t)
                three(b_h[:, :], xT_hi, xT_lo, lambda k: w1_hi[:, bass.ds(e * (HC * F) + k * F, F)],
                      lambda k: w1_lo[:, bass.ds(e * (HC * F) + k * F, F)], None, True).then_inc(s["h_ready"], 1)

            def turn_h(t):
                pe.wait_ge(s["gelu_done"], t + 1)
                if not (isinstance(t, int) and t == 0):
                    pe.wait_ge(s["hmT_sb"], t)
                for k in range(FC):
                    mm = pe.transpose(b_t[:, k * P:(k + 1) * P], hm[:, k * P:(k + 1) * P], ident[:, :])
                mm.then_inc(s["hT2_ready"], 1)

            def down(t, i):
                e = pe.value_load(tab[0:1, bass.ds(t, 1)], min_val=0, max_val=E - 1)
                pe.wait_ge(s["hmT_sb"], t + 1)
                if not (isinstance(t, int) and t == 0):
                    pe.wait_ge(s["y_sb"], t)
                for k in range(FC):
                    mm = pe.matmul(b_y[:, 0:H], hmT[:, i, k * P:(k + 1) * P], w2_s[:, bass.ds(e * (FC * H) + k * H, H)],
                                   start=(k == 0), stop=(k == FC - 1))
                mm.then_inc(s["y_ready"], 1)

            pe.wait_ge(s["w1_lo_ready"], E)
            pe.wait_ge(s["w2_in"], 16)
            turn_in(0, 0, 16)
            up(0)
            turn_in(1, 1, 16)
            turn_h(0)
            with pe.Fori(0, (TILES - 3) // 2) as n:
                for i in range(2):
                    t = 2 * n + 1 + i
                    up(t)
                    turn_in(t + 1, i, 16 * (n + 1) + 16 * 1)
                    down(t - 1, i)
                    turn_h(t)
            for t in range(TILES - 2, TILES):
                up(t)
                if t + 1 < TILES:
                    turn_in(t + 1, (t + 1) % 2, 16 * ((t + 1) // 2 + 1))
                down(t - 1, (t - 1) % 2)
                turn_h(t)
            down(TILES - 1, (TILES - 1) % 2)


_INS = ["x", "condB_zX", "condB_zY", "condB_zR", "L0_ffn_ln1_w", "L0_ffn_ln1_b", "L0_ffn_in_proj_w",
        "L0_ffn_in_proj_b", "L0_ffn_out_proj_w", "L0_ffn_out_proj_b", "L0_ffn_ln2_w", "L0_ffn_ln2_b",
        "L0_ffn_router_w", "L0_ffn_w1", "L0_ffn_w2"]


def kernel(**inputs):
    import numpy as np
    import concourse.bacc as bacc
    from concourse.bass_utils import run_bass_kernel_spmd

    nc = bacc.Bacc("TRN2", target_bir_lowering=False, num_devices=1)
    arrays, args = {}, []
    for name in _INS:
        a = np.ascontiguousarray(inputs[name])
        arrays[f"in_{name}_dram"] = a
        args.append(nc.dram_tensor(f"in_{name}_dram", a.shape, mybir.dt.from_np(a.dtype), kind="ExternalInput").ap())
    out = nc.dram_tensor("out_dram", inputs["x"].shape, F32, kind="ExternalOutput").ap()
    adaln_moe_block(nc, *args, out)
    r = run_bass_kernel_spmd(nc, [arrays], core_ids=[0])
    return r.results[0]["out_dram"]
```

```python
from contextlib import ExitStack

import concourse.bass as bass
from concourse import mybir

P = 128
F32 = mybir.dt.float32
F32R = mybir.dt.float32r
BF16 = mybir.dt.bfloat16
I32 = mybir.dt.int32
U32 = mybir.dt.uint32
ALU = mybir.AluOpType
ACT = mybir.ActivationFunctionType
AX = mybir.AxisListType.X
EPS = 1e-5


def adaln_moe_block(nc, x, zX, zY, zR, ln1_w, ln1_b, in_w, in_b, out_w, out_b, ln2_w, ln2_b,
                    router_w, w1, w2, out):
    S, B, H = x.shape
    NH, D = 16, H // 16
    E, _, F = w1.shape
    HC, FC = H // P, F // P
    G = B // P * S
    TILES = 2 * S + E - 1
    SCALE = float(D) ** -0.5
    DU = 5
    TP = 4
    NPV = 3

    ctx = ExitStack()
    with ctx:
        def sb(name, shape, dt=F32):
            return ctx.enter_context(nc.sbuf_tensor(name, shape, dt))

        def psum(name):
            return ctx.enter_context(nc.psum_tensor(name, [P, 512], F32))

        def sem(name):
            return ctx.enter_context(nc.semaphore(name))

        def pair(name):
            return [sem(f"{name}{i}") for i in range(2)]

        hn2_d = nc.dram_tensor("hn2_d", [P, G, H], F32).ap()
        x1_d = nc.dram_tensor("x1_d", [P, G, H], F32).ap()
        xs_d = nc.dram_tensor("xs_d", [2 * TILES * P, H], F32).ap()
        ys_d = nc.dram_tensor("ys_d", [2 * TILES * P, H], F32).ap()

        ident = sb("ident", [P, P])
        ones_r = sb("ones_r", [2, P], F32R)
        lower = sb("lower", [P, P], BF16)
        ones_b = sb("ones_b", [P, P], BF16)
        iota_i = sb("iota_i", [P, TILES], I32)
        iota_t = sb("iota_t", [P, TILES])
        ln = sb("ln", [P, 4, HC])
        z = sb("z", [P, 3, S])
        alpha = sb("alpha", [P, 2, S])
        wqkv = sb("wqkv", [P, HC, 3 * H])
        wo = sb("wo", [P, HC, H])
        bias = sb("bias", [2, 4 * H], F32R)
        wr = sb("wr", [P, HC * E])
        w1_hi = sb("w1_hi", [P, E * HC * F], F32R)
        w1_lo = sb("w1_lo", [P, E * HC * F], F32R)
        w2_s = sb("w2_s", [P, E * FC * H])
        kv = sb("kv", [P, 2 * S, H])
        xp = sb("xp", [P, 2, H + 2])
        xud = sb("xud", [P, 2, 2, H])
        du = sb("du", [P, DU, H])
        hn = sb("hn", [P, 2, 2, H])
        hT = sb("hT", [P, HC, P])
        aT = sb("aT", [P, HC, P])
        h2T = sb("h2T", [P, HC, P])
        q = sb("q", [P, 2, H])
        qk_prod = sb("qk_prod", [P, 2, TP * H])
        pv_prod = sb("pv_prod", [P, NPV, TP * H])
        sc = sb("sc", [P, NH * S])
        pr = sb("pr", [P, NH * S])
        x1 = sb("x1", [P, 2, H])
        small = sb("small", [P, 64])
        mv = sb("mv", [P, 2, 2])
        rstd = sb("rstd", [P, 3])
        logits = sb("logits", [P, S, E])
        top8 = sb("top8", [P, G, 8])
        idx8 = sb("idx8", [P, S, 8], U32)
        idxf = sb("idxf", [P, S, 2])
        smalli = sb("smalli", [P, 8], I32)
        chosen = sb("chosen", [P, S * E], BF16)
        slot = sb("slot", [P, 2, G], U32)
        tab = sb("tab", [P, 2 * TILES], I32)
        rows = sb("rows", [P, 2, H])
        xin = sb("xin", [P, 2, H])
        xT = sb("xT", [P, HC * P])
        xT_hi = sb("xT_hi", [P, HC, P], F32R)
        xT_lo = sb("xT_lo", [P, HC, P], F32R)
        hm = sb("hm", [P, F])
        hmT = sb("hmT", [P, F])
        y = sb("y", [P, 2, H])

        b_tr, b_qk, b_v, b_at, b_x, b_h, b_t, b_y = [psum(n) for n in
            ("b_tr", "b_qk", "b_v", "b_at", "b_x", "b_h", "b_t", "b_y")]

        names = """const_ready params_in z_in win_in bias_in wT_ready wT_sb wr_sb bias_split bias_lo_in alpha_ready
            w1_hi_ready w1_lo_ready w2_in zero_ready zero_done
            sums_ready scaled du_ready stats1 stats2 rstd1 rstd2 xhat1 xhat2 hT_ready hT_sb h2T_ready h2T_sb
            qkv_ready qkv_sb sc_ready exp_ready pv_piece pv_used aT_sb o_ready x1_ready lg_ready lg_sb
            rt_sub rt_exp rt_m rt_cum slots_ready
            x_tr xT_sb xT_hi_sb xT_lo_sb h_ready gelu_done hT2_ready hmT_sb y_ready y_sb
            out_ready dve_chain pool_chain""".split()
        s = {n: sem(n) for n in names}
        w1_staged, x_in, x1_stored, hn2_stored, rows_in, scattered, xin_in, y_out = [pair(n) for n in
            ("w1_staged", "x_in", "x1_stored", "hn2_stored", "rows_in", "scattered", "xin_in", "y_out")]
        NC = 4
        gathered, base_in, stored = [[sem(f"{n}{i}") for i in range(NC)] for n in ("gathered", "base_in", "stored")]

        wraw = kv[:, 0:8, :]
        w1raw = kv[:, 8:16, :]
        wrraw = kv[0:E, 16, :]
        braw = kv[0:1, 17:21, :]
        blo = w1_lo[0:1, (E - 1) * HC * F:E * HC * F]
        gbuf = kv[:, 0:2 * NC, :].rearrange("p (i k) h -> p i k h", k=2)
        x1buf = kv[:, 8:8 + NC, :]
        xbuf = kv[:, 12:12 + NC, :]
        obuf = kv[:, 16:16 + NC, :]

        rt = qk_prod[:, 0, 0:4 * S * E].rearrange("p (a n) -> p a n", a=4)

        NPIECE = [(g % S) // TP + 1 for g in range(G)]
        PIECES = [sum(NPIECE[:g]) for g in range(G + 1)]

        ROUTE0 = S + 1
        SCATTER = {ROUTE0 + 1: range(0, 6), ROUTE0 + 2: range(6, 12), ROUTE0 + 3: range(12, S)}
        PLACES = {2: (0, 2), 3: (0, 1, 3)}
        SLOTS = {}
        at = -1
        for g, k in zip(range(ROUTE0 + 4, G), [2, 2, 2, 3, 3, 3, 3, 3, 3, 3]):
            for place in PLACES[k]:
                SLOTS[g, place] = at
                at += 1
        LEFT = range(at, TILES)
        NPLACES = 2 + S // TP

        QKV_EARLY = 6

        ZT = 6
        ZEROS = [(t, min(ZT, 2 * TILES - t)) for t in range(0, 2 * TILES, ZT)]
        ZERO_FROM = 2
        W2_FROM = 8

        def rows_left(g, n):
            return n - n // 2 if g >= S else n

        def half_of(g):
            return g // S, g % S

        block = ctx.enter_context(nc.Block())

        @block.sync
        def _(sp):
            def col(a):
                return a.rearrange("(k p) -> p k", p=P)

            for i, a in enumerate((zX, zY, zR)):
                sp.dma_start(z[:, i, :], a.rearrange("(o n) -> o n", o=1).to_broadcast([P, S])).then_inc(s["z_in"], 16)

            def load(g):
                c, p = half_of(g)
                i = g % 2
                if g >= 2:
                    sp.wait_ge(s["du_ready"], g - 1)
                sp.dma_start(xp[:, i, 1:H + 1], x[p, c * P:(c + 1) * P, :]).then_inc(x_in[i], 16)
                up, dn = xud[:, i, 0, :], xud[:, i, 1, :]
                if c == 0:
                    sp.dma_start(up[0:1, :], x[p, 1:2, :]).then_inc(x_in[i], 16)
                    sp.dma_start(up[1:P, :], x[p, 0:P - 1, :]).then_inc(x_in[i], 16)
                    sp.dma_start(dn, x[p, 1:P + 1, :]).then_inc(x_in[i], 16)
                else:
                    sp.dma_start(up, x[p, c * P - 1:(c + 1) * P - 1, :]).then_inc(x_in[i], 16)
                    sp.dma_start(dn[0:P - 1, :], x[p, c * P + 1:(c + 1) * P, :]).then_inc(x_in[i], 16)
                    sp.dma_start(dn[P - 1:P, :], x[p, B - 2:B - 1, :]).then_inc(x_in[i], 16)

            load(0)
            sp.dma_start(wraw[:, 0:6, :], in_w.rearrange("(t p) h -> p t h", p=P)).then_inc(s["win_in"], 16)
            sp.dma_start(wraw[:, 6:8, :], out_w.rearrange("(t p) h -> p t h", p=P)).then_inc(s["win_in"], 16)
            sp.dma_start(wrraw, router_w).then_inc(s["win_in"], 16)
            load(1)
            for i, a in enumerate((ln1_w, ln1_b, ln2_w, ln2_b)):
                sp.dma_start(ln[:, i, :], col(a), allow_slow_non_contiguous=True).then_inc(s["params_in"], 16)
            sp.dma_start(braw[:, 0:3, :], in_b.rearrange("(o t h) -> o t h", o=1, h=H)).then_inc(s["bias_in"], 16)
            sp.dma_start(braw[:, 3:4, :], out_b.rearrange("(o t h) -> o t h", o=1, h=H)).then_inc(s["bias_in"], 16)

            def stage_w1(e):
                if e >= 2:
                    sp.wait_ge(s["w1_lo_ready"], e - 1)
                sp.dma_start(w1raw[:, 4 * (e % 2):4 * (e % 2) + 4, :].rearrange("p (k u) h -> p k (u h)", k=HC),
                             w1[e].rearrange("(k p) f -> p k f", p=P)).then_inc(w1_staged[e % 2], 16)

            stage_w1(0)
            stage_w1(1)
            sp.wait_ge(s["bias_split"], 2)
            sp.dma_start(bias[1:2, :].bitcast(F32), blo.bitcast(F32)).then_inc(s["bias_lo_in"], 16)

            def tile_in(j, i, waits=True):
                if waits:
                    sp.wait_ge(s["x_tr"], j - 1)
                sp.dma_start(xin[:, i, :], xs_d[bass.ds(j * P, P), :]).then_inc(xin_in[i], 16)

            def rows_back(g):
                i = g % 2
                if g >= 2:
                    sp.wait_ge(scattered[i], 32 * (g // 2))
                sp.dma_start(rows[:, i, :], hn2_d[:, g, :]).then_inc(rows_in[i], 16)

            def slot_at(g, place):
                t = SLOTS.get((g, place))
                if t == -1:
                    for i in range(2):
                        sp.wait_ge(scattered[i], 16 * S)
                    tile_in(0, 0, False)
                    tile_in(1, 1, False)
                if t is not None and t + 3 < TILES:
                    tile_in(t + 3, (t + 3) % 2)

            for g in range(-3, G + 2):
                if 2 <= g + 4 < G:
                    load(g + 4)
                if 2 <= g + 3 < E:
                    stage_w1(g + 3)
                if 0 <= g - ZERO_FROM < len(ZEROS):
                    if g == ZERO_FROM:
                        sp.wait_ge(s["zero_ready"], 1)
                    t, n = ZEROS[g - ZERO_FROM]
                    sp.dma_start(xs_d[t * P:(t + n) * P, :].rearrange("(t p) h -> p t h", p=P),
                                 rows[:, 0:1, :].to_broadcast([P, n, H])).then_inc(s["zero_done"], 16)
                if 0 <= g - W2_FROM < E:
                    e = g - W2_FROM
                    sp.dma_start(w2_s[:, e * FC * H:(e + 1) * FC * H].rearrange("p (k h) -> p k h", k=FC),
                                 w2[e].rearrange("(k p) h -> p k h", p=P)).then_inc(s["w2_in"], 16)
                if g - 2 >= 0:
                    sp.wait_ge(s["xhat2"], g - 1)
                    sp.dma_start(hn2_d[:, g - 2, :], hn[:, 1, g % 2, :]).then_inc(hn2_stored[g % 2], 16)
                slot_at(g, 0)
                if 0 <= g - 1 < G:
                    sp.wait_ge(s["x1_ready"], g)
                    sp.dma_start(x1_d[:, g - 1, :], x1[:, (g - 1) % 2, :]).then_inc(x1_stored[(g - 1) % 2], 16)
                for r in SCATTER.get(g, ()):
                    if r == 0:
                        sp.wait_ge(s["zero_done"], 16 * len(ZEROS))
                        for i in range(2):
                            sp.wait_ge(hn2_stored[i], 16 * (S // 2))
                    rows_back(r)
                for place in range(1, NPLACES):
                    slot_at(g, place)
            for i in range(2):
                sp.wait_ge(hn2_stored[i], 16 * S)
            later = [t + 3 for t in LEFT if t + 3 < TILES]
            for j in later[:3]:
                tile_in(j, j % 2)
            for r in range(S):
                rows_back(S + r)
                if r % 2 == 1 and later[3:]:
                    j = later.pop(3)
                    tile_in(j, j % 2)
            for j in later[3:]:
                tile_in(j, j % 2)
            for i in range(2):
                sp.wait_ge(scattered[i], 32 * S)
            J = TILES
            tile_in(J, J % 2)
            tile_in(J + 1, (J + 1) % 2)
            tile_in(J + 2, J % 2)

            def combine_in(g):
                c, p = half_of(g)
                i = g % NC
                if g >= NC:
                    sp.wait_ge(s["out_ready"], g - NC + 1)
                sp.dma_start(x1buf[:, i, :], x1_d[:, g, :]).then_inc(base_in[i], 16)
                sp.dma_start(xbuf[:, i, :], x[p, c * P:(c + 1) * P, :]).then_inc(base_in[i], 16)

            def combine_out(g):
                c, p = half_of(g)
                sp.wait_ge(s["out_ready"], g + 1)
                sp.dma_start(out[p, c * P:(c + 1) * P, :], obuf[:, g % NC, :]).then_inc(stored[g % NC], 16)

            for i in range(2):
                sp.wait_ge(x1_stored[i], 16 * S)
            sp.wait_ge(s["pv_piece"], PIECES[G])
            for g in range(NC):
                combine_in(g)
            for g in range(S):
                with sp.Fori(0, 1) as n:
                    for i in range(2):
                        tile_in(n * 2 + (J + 3 + 2 * g + i), (J + 1 + i) % 2)
                if g >= 1:
                    combine_in(g - 1 + NC)
                    combine_out(g - 1)
            for t in range(2 * S + 3, TILES):
                tile_in(J + t, (J + t) % 2)
            for g in range(S - 1, G):
                if g + NC < G:
                    combine_in(g + NC)
                combine_out(g)
            for i in range(NC):
                sp.wait_ge(stored[i], 16 * (G // NC))

        @block.gpsimd
        def _(pool):
            n = [0]

            def link(ins):
                n[0] += 1
                ins.then_inc(s["pool_chain"], 1)
                pool.wait_ge(s["pool_chain"], n[0])

            link(pool.memset(rstd[:, 2:3], -0.5))
            link(pool.memset(ident[:, :], 0.0))
            pool.affine_select(out=ident[:, :], in_=ident[:, :], compare_op=ALU.not_equal, fill=1.0, base=0,
                               pattern=[[-1, P]], channel_multiplier=1).then_inc(s["const_ready"], 1)
            pool.wait_ge(s["z_in"], 16 * 3)
            link(pool.tensor_tensor(alpha[:, 0, :], z[:, 0, :], z[:, 1, :], ALU.add))
            link(pool.tensor_scalar(alpha[:, 0, :], alpha[:, 0, :], -2.0, None, ALU.mult))
            link(pool.tensor_tensor(alpha[:, 0, :], alpha[:, 0, :], z[:, 2, :], ALU.add))
            pool.tensor_scalar(alpha[:, 1, :], z[:, 2, :], -1.0, None, ALU.mult).then_inc(s["alpha_ready"], 1)

            def later_constants():
                link(pool.memset(ones_b[:, :], 1.0))
                pool.affine_select(out=lower[:, :], in_=ones_b[:, :], compare_op=ALU.is_gt, fill=0.0, base=0,
                                   pattern=[[1, P]], channel_multiplier=-1).then_inc(s["const_ready"], 1)
                pool.memset(ones_r[:, :].bitcast(F32), 1.0).then_inc(s["const_ready"], 1)
                pool.memset(rows[:, 0, :], 0.0).then_inc(s["zero_ready"], 1)
                link(pool.iota(iota_i[:, :], [[1, TILES]], base=0, channel_multiplier=0))
                pool.tensor_copy(iota_t[:, :], iota_i[:, :]).then_inc(s["const_ready"], 1)

            def w1_low(e):
                if e == E - 1:
                    pool.wait_ge(s["bias_lo_in"], 16)
                pool.wait_ge(s["w1_hi_ready"], e + 1)
                part = slice(e * HC * F, (e + 1) * HC * F)
                pool.tensor_tensor(w1_lo[:, part], w1raw[:, 4 * (e % 2):4 * (e % 2) + 4, :].rearrange("p a h -> p (a h)"),
                                   w1_hi[:, part].bitcast(F32), ALU.subtract).then_inc(s["w1_lo_ready"], 1)

            def neighbours(g):
                i = g % 2
                pool.wait_ge(x_in[i], 64 * (g // 2 + 1))
                link(pool.tensor_copy(xp[:, i, 0:H + 2:H + 1], xp[:, i, 2:H:H - 3]))
                link(pool.tensor_tensor(xud[:, i, 0, :], xud[:, i, 0, :], xud[:, i, 1, :], ALU.add))
                pool.tensor_tensor(xud[:, i, 1, :], xp[:, i, 0:H], xp[:, i, 2:H + 2], ALU.add).then_inc(s["sums_ready"], 1)

            def diffuse(g):
                i = g % 2
                d = du[:, g % DU, :]
                pool.wait_ge(s["scaled"], 3 * (g + 1))
                link(pool.tensor_tensor(d, d, xp[:, i, 1:H + 1], ALU.mult))
                link(pool.tensor_tensor(d, d, xud[:, i, 0, :], ALU.add))
                pool.tensor_tensor(d, d, xud[:, i, 1, :], ALU.add).then_inc(s["du_ready"], 1)

            def deviation(g, k):
                pool.wait_ge(s[("stats1", "stats2")[k]], g + 1)
                link(pool.tensor_scalar(rstd[:, k:k + 1], mv[:, k, 1:2], EPS, None, ALU.add))
                pool.tensor_tensor(rstd[:, k:k + 1], rstd[:, k:k + 1], rstd[:, 2:3], ALU.pow).then_inc(s[("rstd1", "rstd2")[k]], 1)

            def scatter(g):
                pool.wait_ge(rows_in[g % 2], 16 * (g // 2 + 1))
                for k in range(2):
                    pool.indirect_dma_start(xs_d, bass.IndirectOffsetOnAxis(ap=slot[:, k, g:g + 1], axis=0),
                                            rows[:, g % 2, :], None).then_inc(scattered[g % 2], 16)

            def gather(g):
                i = g % NC
                if g >= NC:
                    pool.wait_ge(s["out_ready"], g - NC + 1)
                for k in range(2):
                    pool.indirect_dma_start(gbuf[:, i, k, :], None, ys_d[0:(g // S + 1) * TILES * P, :],
                                            bass.IndirectOffsetOnAxis(ap=slot[:, k, g:g + 1], axis=0)).then_inc(gathered[i], 16)

            def low(j):
                pool.wait_ge(s["xT_hi_sb"], j + 1)
                pool.tensor_tensor(xT_lo[:, :, :].rearrange("p k b -> p (k b)"), xT[:, :],
                                   xT_hi[:, :, :].rearrange("p k b -> p (k b)").bitcast(F32), ALU.subtract).then_inc(s["xT_lo_sb"], 1)

            def slot_at(g, place):
                t = SLOTS.get((g, place))
                if t == -1:
                    low(0)
                if t is not None:
                    low(t + 2)

            for g in range(-3, G + 2):
                if 0 <= g + 2 < G:
                    deviation(g + 2, 0)
                if g + 3 < G:
                    neighbours(g + 3)
                slot_at(g, 0)
                if 0 <= g - 1 < G:
                    deviation(g - 1, 1)
                slot_at(g, 1)
                slot_at(g, 2)
                if g + 3 < G:
                    diffuse(g + 3)
                if g == -3:
                    later_constants()
                if 0 <= g + 1 < E:
                    w1_low(g + 1)
                if g == ROUTE0 + 1:
                    pool.wait_ge(s["slots_ready"], 1)
                    pool.wait_ge(s["zero_done"], 16 * len(ZEROS))
                for place in range(3, NPLACES):
                    slot_at(g, place)
                for r in SCATTER.get(g, ()):
                    scatter(r)
            later = [t + 2 for t in LEFT if t + 2 < TILES]
            for j in later[:3]:
                low(j)
            pool.wait_ge(s["slots_ready"], 2)
            for r in range(S):
                scatter(S + r)
                if r % 2 == 1 and later[3:]:
                    low(later.pop(3))
            for j in later[3:]:
                low(j)
            pool.wait_ge(y_out[0], 16 * ((TILES + 1) // 2))
            pool.wait_ge(y_out[1], 16 * (TILES // 2))
            pool.wait_ge(s["pv_piece"], PIECES[G])
            for g in range(S):
                gather(g)
            pool.wait_ge(y_out[0], 16 * TILES)
            pool.wait_ge(y_out[1], 16 * TILES)
            for g in range(S, G):
                gather(g)

        @block.scalar
        def _(act):
            def flat(t):
                return t[:, :, :].rearrange("p k b -> p (k b)")

            def scale(g):
                i, p = g % 2, g % S
                if g == 0:
                    act.wait_ge(s["alpha_ready"], 1)
                if g >= DU:
                    act.wait_ge(s["x1_ready"], g - DU + 1)
                act.wait_ge(x_in[i], 64 * (g // 2 + 1))
                act.activation(du[:, g % DU, :], xp[:, i, 1:H + 1], ACT.Identity, bias=alpha[:, 0, p:p + 1],
                               scale=alpha[:, 1, p:p + 1]).then_inc(s["scaled"], 1)
                act.wait_ge(s["sums_ready"], g + 1)
                act.activation(xud[:, i, 0, :], xud[:, i, 0, :], ACT.Copy, scale=z[:, 1, p:p + 1]).then_inc(s["scaled"], 1)
                act.activation(xud[:, i, 1, :], xud[:, i, 1, :], ACT.Copy, scale=z[:, 0, p:p + 1]).then_inc(s["scaled"], 1)

            def affine(dst, bank, k):
                for c in range(HC):
                    ins = act.activation(dst[:, c * P:(c + 1) * P], bank[:, c * P:(c + 1) * P], ACT.Identity,
                                         scale=ln[:, 2 * k, c:c + 1], bias=ln[:, 2 * k + 1, c:c + 1])
                return ins

            def setup():
                for k in range(HC):
                    qk_bank, vo_bank = ((b_x, b_h), (b_t, b_y))[k]
                    act.wait_ge(s["wT_ready"], 2 * k + 1)
                    act.activation(wqkv[:, k, 0:2 * H], qk_bank[:, :], ACT.Copy).then_inc(s["wT_sb"], 1)
                    act.wait_ge(s["wT_ready"], 2 * k + 2)
                    act.activation(wqkv[:, k, 2 * H:3 * H], vo_bank[:, 0:H], ACT.Copy).then_inc(s["wT_sb"], 1)
                    act.activation(wo[:, k, :], vo_bank[:, H:2 * H], ACT.Copy).then_inc(s["wT_sb"], 1)
                act.wait_ge(s["wT_ready"], 5)
                act.activation(wr[:, :], b_at[:, 0:HC * E], ACT.Copy).then_inc(s["wr_sb"], 1)
                act.wait_ge(s["bias_in"], 32)
                act.activation(bias[0:1, :], braw.rearrange("o a h -> o (a h)"), ACT.Copy).then_inc(s["bias_split"], 1)

            def w1_high(e):
                act.wait_ge(w1_staged[e % 2], 16 * (e // 2 + 1))
                part = slice(e * HC * F, (e + 1) * HC * F)
                act.activation(w1_hi[:, part], w1raw[:, 4 * (e % 2):4 * (e % 2) + 4, :].rearrange("p a h -> p (a h)"),
                               ACT.Copy).then_inc(s["w1_hi_ready"], 1)

            def turned_in(j):
                act.wait_ge(s["x_tr"], j + 1)
                affine(xT, b_x, 1).then_inc(s["xT_sb"], 1)
                act.wait_ge(s["xT_sb"], j + 1)
                act.activation(flat(xT_hi), xT[:, :], ACT.Copy).then_inc(s["xT_hi_sb"], 1)

            def gelu(j):
                act.wait_ge(s["h_ready"], j + 1)
                act.activation(hm[:, :], b_h[:, :], ACT.Gelu).then_inc(s["gelu_done"], 1)

            def turned_h(j):
                act.wait_ge(s["hT2_ready"], j + 1)
                act.activation(hmT[:, :], b_t[:, :], ACT.Copy).then_inc(s["hmT_sb"], 1)

            def store(j, i):
                act.wait_ge(s["y_sb"], j + 1)
                act.dma_start(ys_d[bass.ds(j * P, P), :], y[:, i, :]).then_inc(y_out[i], 16)

            def result(j):
                act.wait_ge(s["y_ready"], j + 1)
                if j >= 2:
                    act.wait_ge(y_out[j % 2], 16 * (j // 2))
                act.activation(y[:, j % 2, :], b_y[:, 0:H], ACT.Copy).then_inc(s["y_sb"], 1)

            def slot_of(t, c=0):
                j = c * TILES + t
                if t == -1:
                    turned_in(j + 1)
                if t >= 0:
                    turned_h(j)
                if t >= 1 and c == 0:
                    result(j - 1)
                if t + 1 < TILES:
                    gelu(j + 1)
                if t >= 1:
                    store(j - 1, (j - 1) % 2)
                if t + 2 < TILES:
                    turned_in(j + 2)
                if t == TILES - 1:
                    if c == 0:
                        result(j)
                    store(j, j % 2)

            def slot_at(g, place):
                if (g, place) in SLOTS:
                    slot_of(SLOTS[g, place])

            def queries_keys_values(g):
                p = g % S
                act.wait_ge(s["qkv_ready"], g + 1)
                act.activation(q[:, g % 2, :], b_qk[:, 0:H], ACT.Copy).then_inc(s["qkv_sb"], 1)
                if p == 8:
                    act.wait_ge(s["w1_lo_ready"], E)
                if p == 0 and g > 0:
                    act.wait_ge(s["sc_ready"], g)
                act.activation(kv[:, p, :], b_qk[:, H:2 * H], ACT.Copy).then_inc(s["qkv_sb"], 1)
                if p == 0 and g > 0:
                    act.wait_ge(s["pv_piece"], PIECES[g])
                act.activation(kv[:, S + p, :], b_v[:, 0:H], ACT.Copy).then_inc(s["qkv_sb"], 1)

            for g in range(-3, G + 2):
                if 0 <= g - 1 < G:
                    act.wait_ge(s["pv_used"], PIECES[g])
                    if g - 1 >= 1:
                        act.wait_ge(s["o_ready"], g - 1)
                    act.activation(flat(aT), b_at[:, 0:H], ACT.Copy).then_inc(s["aT_sb"], 1)
                if g - 2 >= 0:
                    act.wait_ge(s["h2T_ready"], g - 1)
                    if g - 2 >= 1:
                        act.wait_ge(s["lg_ready"], g - 2)
                    affine(flat(h2T), b_tr, 1).then_inc(s["h2T_sb"], 1)
                if g == -3:
                    scale(0)
                    setup()
                early = g >= 0 and QKV_EARLY <= g % S < S - 1
                if early:
                    queries_keys_values(g + 1)
                slot_at(g, 0)
                if 0 <= g < G:
                    n = NH * (g % S + 1)
                    act.wait_ge(s["sc_ready"], g + 1)
                    act.activation(pr[:, 0:n], sc[:, 0:n], ACT.Exp, scale=SCALE).then_inc(s["exp_ready"], 1)
                if 0 < g + 3 < G:
                    scale(g + 3)
                if 0 <= g + 1 < G and not early:
                    queries_keys_values(g + 1)
                if 0 <= g + 2 < E:
                    w1_high(g + 2)
                slot_at(g, 1)
                if 0 <= g + 2 < G:
                    act.wait_ge(s["hT_ready"], g + 3)
                    if g == -2:
                        act.wait_ge(s["params_in"], 16 * 4)
                    if g + 2 >= 1:
                        act.wait_ge(s["qkv_ready"], g + 2)
                    affine(flat(hT), b_tr, 0).then_inc(s["hT_sb"], 1)
                if g - 2 >= 0:
                    act.wait_ge(s["lg_ready"], g - 1)
                    if (g - 2) == S:
                        act.wait_ge(s["rt_sub"], 1)
                    act.activation(logits[:, (g - 2) % S, :], b_tr[:, H:H + E], ACT.Copy).then_inc(s["lg_sb"], 1)
                for place in range(2, NPLACES):
                    slot_at(g, place)
                if g == ROUTE0:
                    act.wait_ge(s["rt_sub"], 1)
                    act.activation(rt[:, 0, :], rt[:, 0, :], ACT.Exp).then_inc(s["rt_exp"], 1)
            act.wait_ge(s["rt_sub"], 2)
            act.activation(rt[:, 0, :], rt[:, 0, :], ACT.Exp).then_inc(s["rt_exp"], 1)
            for t in LEFT:
                slot_of(t)
            slot_of(-1, 1)
            slot_of(0, 1)
            J = TILES
            with act.Fori(0, (TILES - 3) // 2) as n:
                for i in range(2):
                    j = n * 2 + (J + 1 + i)
                    turned_h(j)
                    store(j - 1, (J + i) % 2)
                    gelu(j + 1)
                    turned_in(j + 2)
            slot_of(TILES - 2, 1)
            slot_of(TILES - 1, 1)

        @block.vector
        def _(dve):
            count = [0]

            def tick(ins):
                count[0] += 1
                ins.then_inc(s["dve_chain"], 1)
                return count[0]

            def need(n):
                dve.wait_ge(s["dve_chain"], n)

            def link(ins):
                need(tick(ins))

            def spread(col, n, m):
                return col.rearrange("p (n o) -> p n o", o=1).to_broadcast([P, n, m])

            dve.wait_ge(s["bias_split"], 1)
            dve.tensor_tensor(blo, braw.rearrange("o a h -> o (a h)"), bias[0:1, :].bitcast(F32),
                              ALU.subtract).then_inc(s["bias_split"], 1)

            def unit(src, g, k):
                dve.wait_ge(s[("rstd1", "rstd2")[k]], g + 1)
                if g >= 2:
                    dve.wait_ge(s[("hT_ready", "h2T_ready")[k]], g - 1)
                    if k == 1:
                        dve.wait_ge(hn2_stored[g % 2], 16 * (g // 2))
                dve.tensor_scalar(hn[:, k, g % 2, :], src, mv[:, k, 0:1], rstd[:, k:k + 1], ALU.subtract,
                                  ALU.mult).then_inc(s[("xhat1", "xhat2")[k]], 1)

            def low(j):
                dve.wait_ge(s["xT_hi_sb"], j + 1)
                dve.tensor_tensor(xT_lo[:, :, :].rearrange("p k b -> p (k b)"), xT[:, :],
                                  xT_hi[:, :, :].rearrange("p k b -> p (k b)").bitcast(F32), ALU.subtract).then_inc(s["xT_lo_sb"], 1)

            def result(j):
                dve.wait_ge(s["y_ready"], j + 1)
                dve.wait_ge(y_out[j % 2], 16 * (j // 2))
                dve.tensor_copy(y[:, j % 2, :], b_y[:, 0:H]).then_inc(s["y_sb"], 1)

            def slot_of(t):
                j = TILES + t
                if t == -1:
                    low(j + 1)
                if t + 2 < TILES:
                    low(j + 2)
                if t >= 0:
                    result(j)

            def route(c):
                A, Bv, Cv, Dv = [rt[:, i, :].rearrange("p (g e) -> p g e", e=E) for i in range(4)]
                col = small[:, 0:S]
                link(dve.tensor_reduce(col, logits[:, :, :], AX, ALU.max))
                dve.tensor_tensor(A, logits[:, :, :], spread(col, S, E), ALU.subtract).then_inc(s["rt_sub"], 1)
                dve.wait_ge(s["rt_exp"], c + 1)
                link(dve.tensor_reduce(col, A, AX, ALU.add))
                link(dve.reciprocal(col, col))
                link(dve.tensor_tensor(A, A, spread(col, S, E), ALU.mult))
                for g in range(S):
                    last = dve.max(top8[:, c * S + g, :], A[:, g, :])
                link(last)
                for g in range(S):
                    last = dve.max_index(idx8[:, g, :], top8[:, c * S + g, :], A[:, g, :])
                link(last)
                link(dve.tensor_copy(idxf[:, :, :], idx8[:, :, 0:2]))
                io = iota_t[:, 0:E].rearrange("p (o e) -> p o e", o=1).to_broadcast([P, S, E])
                for k, oh in ((0, A), (1, Bv)):
                    last = dve.tensor_tensor(oh, io, idxf[:, :, k:k + 1].to_broadcast([P, S, E]), ALU.is_equal)
                link(last)
                dve.tensor_tensor(chosen[:, :].rearrange("p (g e) -> p g e", e=E), A, Bv, ALU.add).then_inc(s["rt_m"], 1)
                dve.wait_ge(s["rt_cum"], c + 1)
                bank = (b_x, b_tr)[c]
                cum, tot = [bank[:, i * S * E:(i + 1) * S * E].rearrange("p (g e) -> p g e", e=E) for i in range(2)]
                link(dve.tensor_copy(Cv, tot))
                src, dst, step = Cv, Dv, 1
                while step < S:
                    dve.tensor_copy(dst[:, 0:step, :], src[:, 0:step, :])
                    link(dve.tensor_tensor(dst[:, step:S, :], src[:, step:S, :], src[:, 0:S - step, :], ALU.add))
                    src, dst, step = dst, src, 2 * step
                ones, nt, endt, first = [small[:, 8 * i:8 * i + 8] for i in range(4)]
                nti = smalli[:, 0:8]
                link(dve.tensor_scalar(nti, src[:, S - 1, :], float(P - 1), None, ALU.add))
                link(dve.tensor_scalar(nti, nti, 7, None, ALU.arith_shift_right))
                dve.memset(ones, 1.0)
                link(dve.tensor_copy(nt, nti))
                link(dve.tensor_tensor_scan(endt, ones, nt, 0.0, ALU.mult, ALU.add))
                link(dve.tensor_tensor(first, endt, nt, ALU.subtract))
                link(dve.tensor_scalar(first, first, float(P), float(c * TILES * P), ALU.mult, ALU.add))
                link(dve.tensor_tensor(dst, src, tot, ALU.subtract))
                link(dve.tensor_tensor(dst, dst, cum, ALU.add))
                link(dve.tensor_tensor(dst, dst, first.rearrange("p (o e) -> p o e", o=1).to_broadcast([P, S, E]), ALU.add))
                for k, oh in ((0, A), (1, Bv)):
                    link(dve.tensor_tensor(oh, oh, dst, ALU.mult))
                    link(dve.tensor_reduce(idxf[:, :, k], oh, AX, ALU.add))
                    link(dve.tensor_copy(slot[:, k, c * S:(c + 1) * S], idxf[:, :, k]))
                tt = qk_prod[:, 1, 0:TILES * E].rearrange("p (t e) -> p t e", e=E)
                te = qk_prod[:, 1, TILES * E:TILES * (E + 1)]
                link(dve.tensor_tensor(tt, spread(iota_t[:, :], TILES, E),
                                       endt.rearrange("p (o e) -> p o e", o=1).to_broadcast([P, TILES, E]), ALU.is_ge))
                link(dve.tensor_reduce(te, tt, AX, ALU.add))
                link(dve.tensor_scalar(te, te, float(E - 1), None, ALU.min))
                dve.tensor_copy(tab[:, c * TILES:(c + 1) * TILES], te).then_inc(s["slots_ready"], 1)

            for g in range(-3, G + 2):
                T = g % S + 1
                if 0 <= g + 2 < G:
                    d = du[:, (g + 2) % DU, :]
                    dve.wait_ge(s["du_ready"], g + 3)
                    st = tick(dve.bn_stats(small[:, 48:54], d))
                aggregated = False

                def aggregate():
                    need(st)
                    if g + 2 >= 1:
                        dve.wait_ge(s["xhat1"], g + 2)
                    dve.bn_aggr(mv[:, 0, :], small[:, 48:54]).then_inc(s["stats1"], 1)

                if 0 <= g < G:
                    scv = sc[:, 0:NH * T].rearrange("p (n t) -> p n t", t=T)
                    dve.wait_ge(s["qkv_sb"], 3 * (g + 1))
                    if g >= 1:
                        dve.wait_ge(s["exp_ready"], g)
                    made, summed = [], []

                    def multiply(m):
                        t0, t1 = m * TP, min(T, m * TP + TP)
                        if m >= 2:
                            need(summed[m - 2])
                        made.append(tick(dve.tensor_tensor(
                            qk_prod[:, m % 2, 0:(t1 - t0) * H].rearrange("p (t h) -> p t h", h=H),
                            q[:, g % 2, :].rearrange("p (o h) -> p o h", o=1).to_broadcast([P, t1 - t0, H]),
                            kv[:, t0:t1, :], ALU.mult)))

                    def add_up(m):
                        t0, t1 = m * TP, min(T, m * TP + TP)
                        need(made[m])
                        summed.append(tick(dve.tensor_reduce(
                            scv.rearrange("p n t -> p t n")[:, t0:t1, :],
                            qk_prod[:, m % 2, 0:(t1 - t0) * H].rearrange("p (t n d) -> p t n d", n=NH, d=D), AX, ALU.add)))

                    for m in range(NPIECE[g]):
                        multiply(m)
                        if m == 0 and g + 2 < G:
                            aggregate()
                            aggregated = True
                        if m >= 1:
                            add_up(m - 1)
                    add_up(NPIECE[g] - 1)
                if 0 <= g + 2 < G and not aggregated:
                    aggregate()
                if 0 <= g < G:
                    need(summed[-1])
                    most = tick(dve.tensor_reduce(small[:, 0:NH], scv, AX, ALU.max))
                if 0 <= g - 1 < G:
                    dve.wait_ge(s["o_ready"], g)
                    if g - 1 >= 2:
                        dve.wait_ge(x1_stored[(g - 1) % 2], 16 * ((g - 1) // 2))
                    dve.tensor_tensor(x1[:, (g - 1) % 2, :], du[:, (g - 1) % DU, :], b_at[:, H:2 * H], ALU.add).then_inc(s["x1_ready"], 1)
                if 0 <= g < G:
                    need(most)
                    dve.tensor_tensor(scv, scv, spread(small[:, 0:NH], NH, T), ALU.subtract).then_inc(s["sc_ready"], 1)
                if 0 <= g - 1 < G:
                    dve.wait_ge(s["x1_ready"], g)
                    link(dve.bn_stats(small[:, 54:60], x1[:, (g - 1) % 2, :]))
                    if g - 1 >= 1:
                        dve.wait_ge(s["xhat2"], g - 1)
                    dve.bn_aggr(mv[:, 1, :], small[:, 54:60]).then_inc(s["stats2"], 1)
                if 0 <= g + 2 < G:
                    unit(du[:, (g + 2) % DU, :], g + 2, 0)
                if 0 <= g < G:
                    dve.wait_ge(s["exp_ready"], g + 1)
                    prv = pr[:, 0:NH * T].rearrange("p (n t) -> p n t", t=T)
                    link(dve.tensor_reduce(small[:, 16:16 + NH], prv, AX, ALU.add))
                    link(dve.reciprocal(small[:, 32:32 + NH], small[:, 16:16 + NH]))
                    link(dve.tensor_tensor(prv, prv, spread(small[:, 32:32 + NH], NH, T), ALU.mult))

                    def value_products(m):
                        t0, t1 = m * TP, min(T, m * TP + TP)
                        at = PIECES[g] + m
                        if at >= NPV:
                            dve.wait_ge(s["pv_used"], at - NPV + 1)
                        ins = dve.tensor_tensor(pv_prod[:, at % NPV, 0:(t1 - t0) * H].rearrange("p (t n d) -> p t n d", n=NH, d=D),
                                                kv[:, S + t0:S + t1, :].rearrange("p t (n d) -> p t n d", d=D),
                                                pr[:, 0:NH * T].rearrange("p (n t o) -> p t n o", t=T, o=1)[:, t0:t1, :, :].to_broadcast([P, t1 - t0, NH, D]),
                                                ALU.mult)
                        if rows_left(g, t1 - t0) == t1 - t0:
                            ins.then_inc(s["pv_piece"], 1)
                            return None
                        return tick(ins)

                    def add_pairs(m, done):
                        n = min(TP, T - m * TP)
                        keep = rows_left(g, n)
                        v = pv_prod[:, (PIECES[g] + m) % NPV, :]
                        need(done)
                        dve.tensor_tensor(v[:, 0:(n - keep) * H], v[:, 0:(n - keep) * H], v[:, keep * H:n * H],
                                          ALU.add).then_inc(s["pv_piece"], 1)

                    last = value_products(0)
                    for m in range(1, NPIECE[g]):
                        if T - m * TP == 1 and last is not None:
                            add_pairs(m - 1, last)
                            last = None
                        this = value_products(m)
                        if last is not None:
                            add_pairs(m - 1, last)
                        last = this
                    if last is not None:
                        add_pairs(NPIECE[g] - 1, last)
                if 0 <= g - 1 < G:
                    unit(x1[:, (g - 1) % 2, :], g - 1, 1)
                if g == ROUTE0:
                    dve.wait_ge(s["const_ready"], 4)
                    dve.wait_ge(s["lg_sb"], S)
                    route(0)
            dve.wait_ge(s["lg_sb"], G)
            route(1)
            slot_of(-1)
            slot_of(0)

            def combine(g):
                i = g % NC
                dve.wait_ge(base_in[i], 32 * (g // NC + 1))
                link(dve.tensor_tensor(x1buf[:, i, :], x1buf[:, i, :], xbuf[:, i, :], ALU.add))
                dve.wait_ge(gathered[i], 32 * (g // NC + 1))
                link(dve.scalar_tensor_tensor(out=x1buf[:, i, :], in0=gbuf[:, i, 0, :], scalar=top8[:, g, 0:1],
                                              in1=x1buf[:, i, :], op0=ALU.mult, op1=ALU.add))
                if g >= NC:
                    dve.wait_ge(stored[i], 16 * (g // NC))
                dve.scalar_tensor_tensor(out=obuf[:, i, :], in0=gbuf[:, i, 1, :], scalar=top8[:, g, 1:2],
                                         in1=x1buf[:, i, :], op0=ALU.mult, op1=ALU.add).then_inc(s["out_ready"], 1)

            for g in range(S):
                for t in range(2 * g + 1, 2 * g + 3):
                    slot_of(t)
                combine(g)
            for t in range(2 * S + 1, TILES):
                slot_of(t)
            for g in range(S, G):
                combine(g)

        @block.tensor
        def _(pe):
            pe.wait_ge(s["const_ready"], 1)
            pe.wait_ge(s["win_in"], 16 * 3)
            for k in range(HC):
                for bank, t0 in (((b_x, b_h), (b_t, b_y))[k][0], 0), (((b_x, b_h), (b_t, b_y))[k][1], 4):
                    for t in range(4):
                        mm = pe.transpose(bank[:, t * P:(t + 1) * P], wraw[:, t0 + t, k * P:(k + 1) * P], ident[:, :])
                    mm.then_inc(s["wT_ready"], 1)
            for k in range(HC):
                mm = pe.transpose(b_at[:, k * E:(k + 1) * E], wrraw[:, k * P:(k + 1) * P], ident[0:E, 0:E])
            mm.then_inc(s["wT_ready"], 1)

            def turn_in(j, i, loads):
                pe.wait_ge(xin_in[i], 16 * loads)
                if not (isinstance(j, int) and j == 0):
                    pe.wait_ge(s["xT_sb"], j)
                for k in range(HC):
                    mm = pe.transpose(b_x[:, k * P:(k + 1) * P], xin[:, i, k * P:(k + 1) * P], ident[:, :])
                mm.then_inc(s["x_tr"], 1)

            def expert(j):
                return pe.value_load(tab[0:1, bass.ds(j, 1)], min_val=0, max_val=E - 1)

            def up(j, e):
                pe.wait_ge(s["xT_lo_sb"], j + 1)
                for k in range(HC):
                    cols = bass.ds(e * (HC * F) + k * F, F)
                    pe.matmul(b_h[:, :], xT_hi[:, k, :], w1_hi[:, cols], start=(k == 0), stop=False)
                    pe.matmul(b_h[:, :], xT_hi[:, k, :], w1_lo[:, cols], start=False, stop=False)
                    mm = pe.matmul(b_h[:, :], xT_lo[:, k, :], w1_hi[:, cols], start=False, stop=(k == HC - 1))
                mm.then_inc(s["h_ready"], 1)

            def turn_h(j):
                pe.wait_ge(s["gelu_done"], j + 1)
                for k in range(FC):
                    mm = pe.transpose(b_t[:, k * P:(k + 1) * P], hm[:, k * P:(k + 1) * P], ident[:, :])
                mm.then_inc(s["hT2_ready"], 1)

            def down(j, e):
                pe.wait_ge(s["hmT_sb"], j + 1)
                if not (isinstance(j, int) and j == 0):
                    pe.wait_ge(s["y_sb"], j)
                for k in range(FC):
                    mm = pe.matmul(b_y[:, 0:H], hmT[:, k * P:(k + 1) * P], w2_s[:, bass.ds(e * (FC * H) + k * H, H)],
                                   start=(k == 0), stop=(k == FC - 1))
                mm.then_inc(s["y_ready"], 1)

            def slot_of(t, c=0):
                j = c * TILES + t
                if t == -1:
                    pe.wait_ge(s["slots_ready"], c + 1)
                    if c == 0:
                        pe.wait_ge(s["w1_lo_ready"], E)
                        pe.wait_ge(s["w2_in"], 16 * E)
                    turn_in(j + 1, (j + 1) % 2, (j + 1) // 2 + 1)
                if t + 1 < TILES:
                    e_next = expert(j + 1)
                if t >= 0:
                    turn_h(j)
                if t + 1 < TILES:
                    up(j + 1, e_next)
                if t >= 0:
                    e = expert(j)
                if t + 2 < TILES:
                    turn_in(j + 2, (j + 2) % 2, (j + 2) // 2 + 1)
                if t >= 0:
                    down(j, e)

            def router(g):
                pe.wait_ge(s["h2T_sb"], g + 1)
                if g + 4 < G:
                    pe.wait_ge(s["hT_sb"], g + 5)
                for k in range(HC):
                    mm = pe.matmul(b_tr[:, H:H + E], h2T[:, k, :], wr[:, k * E:(k + 1) * E], start=(k == 0), stop=(k == HC - 1))
                mm.then_inc(s["lg_ready"], 1)

            def slot_at(g, place):
                if (g, place) in SLOTS:
                    slot_of(SLOTS[g, place])

            for g in range(-2, G + 2):
                if g - 2 >= 0:
                    pe.wait_ge(s["xhat2"], g - 1)
                    if g - 2 >= 1:
                        pe.wait_ge(s["lg_sb"], g - 2)
                    else:
                        pe.wait_ge(s["hT_sb"], g + 2)
                    for k in range(HC):
                        mm = pe.transpose(b_tr[:, k * P:(k + 1) * P], hn[:, 1, g % 2, k * P:(k + 1) * P], ident[:, :])
                    mm.then_inc(s["h2T_ready"], 1)
                if 0 <= g - 1 < G:
                    pe.wait_ge(s["aT_sb"], g)
                    pe.matmul(b_at[:, H:2 * H], ones_r[:, :], bias[:, 3 * H:4 * H], start=True, stop=False)
                    for k in range(HC):
                        mm = pe.matmul(b_at[:, H:2 * H], aT[:, k, :], wo[:, k, :], start=False, stop=(k == HC - 1))
                    mm.then_inc(s["o_ready"], 1)
                if 0 <= g + 1 < G:
                    if g == -1:
                        pe.wait_ge(s["const_ready"], 3)
                        pe.wait_ge(s["wT_sb"], 6)
                        pe.wait_ge(s["wr_sb"], 1)
                        pe.wait_ge(s["bias_lo_in"], 16)
                    pe.wait_ge(s["hT_sb"], g + 2)
                    if g >= 0:
                        pe.wait_ge(s["qkv_sb"], 3 * (g + 1))
                    for bank, a, b in ((b_qk, 0, 2 * H), (b_v, 2 * H, 3 * H)):
                        pe.matmul(bank[:, 0:b - a], ones_r[:, :], bias[:, a:b], start=True, stop=False)
                        for k in range(HC):
                            mm = pe.matmul(bank[:, 0:b - a], hT[:, k, :], wqkv[:, k, a:b], start=False, stop=(k == HC - 1))
                    mm.then_inc(s["qkv_ready"], 1)
                slot_at(g, 0)
                slot_at(g, 1)
                if 0 <= g + 2 < G:
                    pe.wait_ge(s["xhat1"], g + 3)
                    if g - 2 >= 0:
                        pe.wait_ge(s["h2T_sb"], g - 1)
                    elif g + 2 >= 1:
                        pe.wait_ge(s["hT_sb"], g + 2)
                    for k in range(HC):
                        mm = pe.transpose(b_tr[:, k * P:(k + 1) * P], hn[:, 0, g % 2, k * P:(k + 1) * P], ident[:, :])
                    mm.then_inc(s["hT_ready"], 1)
                if 0 <= g < G:
                    T = g % S + 1
                    if g >= 1:
                        pe.wait_ge(s["x1_ready"], g)
                    for m in range(NPIECE[g]):
                        at = PIECES[g] + m
                        n = rows_left(g, min(TP, T - m * TP))
                        pe.wait_ge(s["pv_piece"], at + 1)
                        for t in range(n):
                            for k in range(HC):
                                lo = t * H + k * P
                                mm = pe.matmul(b_at[:, k * P:(k + 1) * P], pv_prod[:, at % NPV, lo:lo + P], ident[:, :],
                                               start=(m == 0 and t == 0 and k == 0), stop=(m == NPIECE[g] - 1 and t == n - 1),
                                               skip_group_check=True)
                        mm.then_inc(s["pv_used"], 1)
                        if m == 0 and g - 2 >= 0:
                            router(g - 2)
                        slot_at(g, 2 + m)
                if g - 2 >= 0 and g >= G:
                    router(g - 2)
                if g == ROUTE0:
                    pe.wait_ge(s["rt_m"], 1)
                    pe.matmul(b_x[:, 0:S * E], lower[:, :], chosen[:, :], start=True, stop=True)
                    pe.matmul(b_x[:, S * E:2 * S * E], ones_b[:, :], chosen[:, :], start=True, stop=True).then_inc(s["rt_cum"], 1)
            for t in LEFT[:2]:
                slot_of(t)
            pe.wait_ge(s["rt_m"], 2)
            pe.matmul(b_tr[:, 0:S * E], lower[:, :], chosen[:, :], start=True, stop=True)
            pe.matmul(b_tr[:, S * E:2 * S * E], ones_b[:, :], chosen[:, :], start=True, stop=True).then_inc(s["rt_cum"], 1)
            for t in LEFT[2:]:
                slot_of(t)
            slot_of(-1, 1)
            slot_of(0, 1)
            J = TILES
            with pe.Fori(0, (TILES - 3) // 2) as n:
                for i in range(2):
                    j = n * 2 + (J + 1 + i)
                    e_next = expert(j + 1)
                    turn_h(j)
                    up(j + 1, e_next)
                    e = expert(j)
                    turn_in(j + 2, (J + 1 + i) % 2, n + ((J + 3 + i) // 2 + 1))
                    down(j, e)
            slot_of(TILES - 2, 1)
            slot_of(TILES - 1, 1)


_INS = ["x", "condB_zX", "condB_zY", "condB_zR", "L0_ffn_ln1_w", "L0_ffn_ln1_b", "L0_ffn_in_proj_w",
        "L0_ffn_in_proj_b", "L0_ffn_out_proj_w", "L0_ffn_out_proj_b", "L0_ffn_ln2_w", "L0_ffn_ln2_b",
        "L0_ffn_router_w", "L0_ffn_w1", "L0_ffn_w2"]


def kernel(**inputs):
    import numpy as np
    import concourse.bacc as bacc
    from concourse.bass_utils import run_bass_kernel_spmd

    nc = bacc.Bacc("TRN2", target_bir_lowering=False, num_devices=1)
    arrays, args = {}, []
    for name in _INS:
        a = np.ascontiguousarray(inputs[name])
        arrays[f"in_{name}_dram"] = a
        args.append(nc.dram_tensor(f"in_{name}_dram", a.shape, mybir.dt.from_np(a.dtype), kind="ExternalInput").ap())
    out = nc.dram_tensor("out_dram", inputs["x"].shape, F32, kind="ExternalOutput").ap()
    adaln_moe_block(nc, *args, out)
    r = run_bass_kernel_spmd(nc, [arrays], core_ids=[0])
    return r.results[0]["out_dram"]
```

```python
from contextlib import ExitStack

import concourse.bass as bass
from concourse import mybir

P = 128
F32 = mybir.dt.float32
F32R = mybir.dt.float32r
BF16 = mybir.dt.bfloat16
I32 = mybir.dt.int32
U32 = mybir.dt.uint32
ALU = mybir.AluOpType
ACT = mybir.ActivationFunctionType
AX = mybir.AxisListType.X
EPS = 1e-5


def adaln_moe_block(nc, x, zX, zY, zR, ln1_w, ln1_b, in_w, in_b, out_w, out_b, ln2_w, ln2_b,
                    router_w, w1, w2, out):
    S, B, H = x.shape
    NH, D = 16, H // 16
    E, _, F = w1.shape
    HC, FC = H // P, F // P
    G = B // P * S
    ENDS = (10, 22, G)
    GROUPS = [range(a, b) for a, b in zip((0,) + ENDS, ENDS)]
    NG = len(GROUPS)
    GMAX = max(len(r) for r in GROUPS)
    NTILES = [2 * len(r) + E - 1 for r in GROUPS]
    FIRST = [sum(NTILES[:r]) for r in range(NG + 1)]
    ALL = FIRST[NG]
    SCALE = float(D) ** -0.5
    DU = 6
    TP = 4
    NPV = 3

    ctx = ExitStack()
    with ctx:
        def sb(name, shape, dt=F32):
            return ctx.enter_context(nc.sbuf_tensor(name, shape, dt))

        def psum(name):
            return ctx.enter_context(nc.psum_tensor(name, [P, 512], F32))

        def sem(name):
            return ctx.enter_context(nc.semaphore(name))

        def pair(name):
            return [sem(f"{name}{i}") for i in range(2)]

        hn2_d = nc.dram_tensor("hn2_d", [P, G, H], F32).ap()
        x1_d = nc.dram_tensor("x1_d", [P, G, H], F32).ap()
        xs_d = nc.dram_tensor("xs_d", [ALL * P, H], F32).ap()
        ys_d = nc.dram_tensor("ys_d", [ALL * P, H], F32).ap()

        ident = sb("ident", [P, P])
        ones_r = sb("ones_r", [2, P], F32R)
        lower = sb("lower", [P, P], BF16)
        ones_b = sb("ones_b", [P, P], BF16)
        iota_i = sb("iota_i", [P, max(NTILES)], I32)
        iota_t = sb("iota_t", [P, max(NTILES)])
        ln = sb("ln", [P, 4, HC])
        z = sb("z", [P, 3, S])
        alpha = sb("alpha", [P, 2, S])
        wqkv = sb("wqkv", [P, HC, 3 * H])
        wo = sb("wo", [P, HC, H])
        bias = sb("bias", [2, 4 * H], F32R)
        wr = sb("wr", [P, HC * E])
        w1_hi = sb("w1_hi", [P, E * HC * F], F32R)
        w1_lo = sb("w1_lo", [P, E * HC * F], F32R)
        w2_s = sb("w2_s", [P, E * FC * H])
        kv = sb("kv", [P, 2 * S, H])
        xp = sb("xp", [P, 2, H + 2])
        xud = sb("xud", [P, 2, 2, H])
        du = sb("du", [P, DU, H])
        hn = sb("hn", [P, 2, 2, H])
        hT = sb("hT", [P, HC, P])
        aT = sb("aT", [P, HC, P])
        h2T = sb("h2T", [P, HC, P])
        q = sb("q", [P, 2, H])
        qk_prod = sb("qk_prod", [P, 2, TP * H])
        pv_prod = sb("pv_prod", [P, NPV, TP * H])
        sc = sb("sc", [P, 2, NH * S])
        pr = sb("pr", [P, 2, NH * S])
        x1 = sb("x1", [P, 2, H])
        small = sb("small", [P, 64])
        junk = sb("junk", [P, 2])
        mv = sb("mv", [P, 2, 2])
        rstd = sb("rstd", [P, 3])
        logits = sb("logits", [P, G, E])
        gates = sb("gates", [P, G, 2])
        top8 = sb("top8", [P, G, 8])
        idx8 = sb("idx8", [P, G, 8], U32)
        idxf = sb("idxf", [P, 2, GMAX])
        smalli = sb("smalli", [P, 8], I32)
        chosen = sb("chosen", [P, GMAX * E], BF16)
        slot_row = sb("slot_row", [P, 2, G], U32)
        tab = sb("tab", [P, ALL], I32)
        zeros = sb("zeros", [P, H])
        rows = sb("rows", [P, 2, H])
        xin_y = sb("xin_y", [P, 4, H])
        xT = sb("xT", [P, HC * P])
        xT_hi = sb("xT_hi", [P, HC, P], F32R)
        xT_lo = sb("xT_lo", [P, HC, P], F32R)
        hm_hmT = sb("hm_hmT", [P, 2 * F])
        xin, y = xin_y[:, 0:2, :], xin_y[:, 2:4, :]
        hm, hmT = hm_hmT[:, 0:F], hm_hmT[:, F:2 * F]

        b_tr, b_qk, b_v, b_at, b_x, b_h, b_t, b_y = [psum(n) for n in
            ("b_tr", "b_qk", "b_v", "b_at", "b_x", "b_h", "b_t", "b_y")]

        names = """const_ready params_in z_in win_in bias_in wT_ready wT_sb wr_sb bias_split bias_lo_in alpha_ready
            w1_hi_ready w1_lo_ready w2_in zero_ready
            sums_ready scaled du_ready stats1 stats2 rstd1 rstd2 xhat1 xhat2 hT_ready hT_sb h2T_ready h2T_sb
            qkv_ready qk_sb v_sb sc_ready exp_ready pv_piece pv_used aT_sb o_ready x1_ready lg_ready lg_sb
            rt_sub rt_exp rt_m rt_cum rt_cum_sb slots_ready
            x_tr xT_sb xT_hi_sb xT_lo_sb h_ready gelu_done hT2_ready hmT_sb y_ready y_sb
            out_ready dve_chain pool_chain""".split()
        s = {n: sem(n) for n in names}
        w1_staged, x_in, x1_stored, hn2_stored, rows_in, scattered, xin_in, y_out = [pair(n) for n in
            ("w1_staged", "x_in", "x1_stored", "hn2_stored", "rows_in", "scattered", "xin_in", "y_out")]
        zero_done = [sem(f"zero_done{i}") for i in range(NG)]
        NC = 4
        gathered, base_in, stored = [[sem(f"{n}{i}") for i in range(NC)] for n in ("gathered", "base_in", "stored")]

        wraw = kv[:, 0:8, :]
        w1raw = [xin_y[:, :, :].rearrange("p a h -> p (a h)"), hm_hmT[:, :]]
        wrraw = kv[0:E, 16, :]
        braw = kv[0:1, 17:21, :]
        blo = w1_lo[0:1, (E - 1) * HC * F:E * HC * F]
        gbuf = kv[:, 0:2 * NC, :].rearrange("p (i k) h -> p i k h", k=2)
        x1buf = kv[:, 8:8 + NC, :]
        xbuf = kv[:, 12:12 + NC, :]
        obuf = kv[:, 16:16 + NC, :]

        NPIECE = [(g % S) // TP + 1 for g in range(G)]
        PIECES = [sum(NPIECE[:g]) for g in range(G + 1)]

        SUMMED = S + 10

        NPLACES = 2 + S // TP
        ROUTE = {GROUPS[r][-1] + 3: r for r in range(NG - 1)}
        PER = 4
        SCATTER = {}
        for g, r in ROUTE.items():
            for i, step in enumerate(GROUPS[r]):
                SCATTER[g + 1 + i // PER, i % PER] = step
        PLACES = {0: (), 1: (0,), 2: (0, 1), 3: (0, 1, 2), 4: (0, 0, 1, 2)}
        LATER = {1: (2,), 2: (3, 4), 3: (2, 3, 4)}
        WANT = [0] * 12 + [1, 1, 1, 2, 3, 1, 3, 2, 2, 2, 2, 2, 3, 3, 1, 3, 3, 3, 3, 3, 1, 1, 1]

        def group_of(j):
            return [r for r in range(NG) if j >= FIRST[r]][-1]

        def scattered_by(r):
            return max([g for (g, n), step in SCATTER.items() if step == GROUPS[r][-1]] + [G + 3 if r == NG - 1 else 0])

        SLOTS = {(g, n): [] for g in range(-3, G + 3) for n in range(NPLACES)}
        at = -1
        for g in range(G + 3):
            for n in (PLACES if g != S else LATER)[WANT[g]]:
                if scattered_by(group_of(max(at + 3, 0))) < g:
                    SLOTS[g, n].append(at)
                    at += 1
        LEFT = range(at, ALL)
        TAIL = LEFT[2]
        COMBINE = FIRST[NG - 1] + 2

        def projected_late(g):
            return g > S

        def diffused_late(g):
            return g >= S

        ZT = 5
        ZEROS = [(t, min(ZT, FIRST[r + 1] - t), r) for r in range(NG) for t in range(FIRST[r], FIRST[r + 1], ZT)]
        W1_FROM = 4
        ZERO_FROM = 2
        W2_FROM = 3

        def rows_left(g, n):
            return n if g < S else 1 if g < SUMMED else n - n // 2

        def slots_before(g):
            share = -(-(ALL - COMBINE) * (g + 1) // GROUPS[NG - 1][0])
            return min(ALL, COMBINE + share)

        LOOPS = (ALL - 2 - (TAIL + 2)) // 2

        def rt(i, n, k=1):
            return qk_prod[:, 0, i * GMAX * E:(i * GMAX + k * n) * E]

        def half_of(g):
            return g // S, g % S

        block = ctx.enter_context(nc.Block())

        @block.sync
        def _(sp):
            def col(a):
                return a.rearrange("(k p) -> p k", p=P)

            for i, a in enumerate((zX, zY, zR)):
                sp.dma_start(z[:, i, :], a.rearrange("(o n) -> o n", o=1).to_broadcast([P, S])).then_inc(s["z_in"], 16)

            def load(g):
                c, p = half_of(g)
                i = g % 2
                if g >= 2:
                    sp.wait_ge(s["du_ready"], g - 1)
                sp.dma_start(xp[:, i, 1:H + 1], x[p, c * P:(c + 1) * P, :]).then_inc(x_in[i], 16)
                up, dn = xud[:, i, 0, :], xud[:, i, 1, :]
                if c == 0:
                    sp.dma_start(up[0:1, :], x[p, 1:2, :]).then_inc(x_in[i], 16)
                    sp.dma_start(up[1:P, :], x[p, 0:P - 1, :]).then_inc(x_in[i], 16)
                    sp.dma_start(dn, x[p, 1:P + 1, :]).then_inc(x_in[i], 16)
                else:
                    sp.dma_start(up, x[p, c * P - 1:(c + 1) * P - 1, :]).then_inc(x_in[i], 16)
                    sp.dma_start(dn[0:P - 1, :], x[p, c * P + 1:(c + 1) * P, :]).then_inc(x_in[i], 16)
                    sp.dma_start(dn[P - 1:P, :], x[p, B - 2:B - 1, :]).then_inc(x_in[i], 16)

            load(0)
            sp.dma_start(braw[:, 0:3, :], in_b.rearrange("(o t h) -> o t h", o=1, h=H)).then_inc(s["bias_in"], 16)
            sp.dma_start(braw[:, 3:4, :], out_b.rearrange("(o t h) -> o t h", o=1, h=H)).then_inc(s["bias_in"], 16)
            sp.dma_start(wraw[:, 0:6, :], in_w.rearrange("(t p) h -> p t h", p=P)).then_inc(s["win_in"], 16)
            sp.dma_start(wraw[:, 6:8, :], out_w.rearrange("(t p) h -> p t h", p=P)).then_inc(s["win_in"], 16)
            sp.dma_start(wrraw, router_w).then_inc(s["win_in"], 16)
            load(1)
            for i, a in enumerate((ln1_w, ln1_b, ln2_w, ln2_b)):
                sp.dma_start(ln[:, i, :], col(a), allow_slow_non_contiguous=True).then_inc(s["params_in"], 16)

            def stage_w1(e):
                if e >= 2:
                    sp.wait_ge(s["w1_lo_ready"], e - 1)
                sp.dma_start(w1raw[e % 2].rearrange("p (k f) -> p k f", k=HC),
                             w1[e].rearrange("(k p) f -> p k f", p=P)).then_inc(w1_staged[e % 2], 16)

            sp.wait_ge(s["bias_split"], 2)
            sp.dma_start(bias[1:2, :].bitcast(F32), blo.bitcast(F32)).then_inc(s["bias_lo_in"], 16)
            stage_w1(0)
            stage_w1(1)

            def tile_in(j):
                if j in FIRST:
                    for i in range(2):
                        sp.wait_ge(scattered[i], 32 * len([g for g in range(ENDS[group_of(j)]) if g % 2 == i]))
                if j >= 2:
                    sp.wait_ge(s["x_tr"], j - 1)
                sp.dma_start(xin[:, j % 2, :], xs_d[j * P:(j + 1) * P, :]).then_inc(xin_in[j % 2], 16)

            def store(j):
                sp.wait_ge(s["y_sb"], j + 1)
                sp.dma_start(ys_d[j * P:(j + 1) * P, :], y[:, j % 2, :]).then_inc(y_out[j % 2], 16)

            def rows_back(g):
                i = g % 2
                sp.wait_ge(hn2_stored[i], 16 * (g // 2 + 1))
                if g >= 2:
                    sp.wait_ge(scattered[i], 32 * (g // 2))
                sp.dma_start(rows[:, i, :], hn2_d[:, g, :]).then_inc(rows_in[i], 16)

            def slot(j):
                if j == -1:
                    tile_in(0)
                    tile_in(1)
                if j + 3 < ALL:
                    tile_in(j + 3)
                if j >= 1:
                    store(j - 1)
                if j == ALL - 1:
                    store(j)

            def place(g, n):
                for j in SLOTS[g, n]:
                    slot(j)

            def refill(g, n):
                if (g, n) in SCATTER:
                    step = SCATTER[g, n]
                    if step == 0:
                        rows_back(0)
                        rows_back(1)
                    rows_back(step + 2)

            for g in range(-3, G + 3):
                if 2 <= g + 4 < G:
                    load(g + 4)
                if 2 <= g - W1_FROM + 1 < E:
                    stage_w1(g - W1_FROM + 1)
                if 0 <= g - ZERO_FROM < len(ZEROS):
                    if g == ZERO_FROM:
                        sp.wait_ge(s["zero_ready"], 1)
                    t, n, r = ZEROS[g - ZERO_FROM]
                    sp.dma_start(xs_d[t * P:(t + n) * P, :].rearrange("(t p) h -> p t h", p=P),
                                 zeros[:, :].rearrange("p (o h) -> p o h", o=1).to_broadcast([P, n, H])).then_inc(zero_done[r], 16)
                if 0 <= g - W2_FROM < E:
                    e = g - W2_FROM
                    sp.dma_start(w2_s[:, e * FC * H:(e + 1) * FC * H].rearrange("p (k h) -> p k h", k=FC),
                                 w2[e].rearrange("(k p) h -> p k h", p=P)).then_inc(s["w2_in"], 16)
                if g - 3 >= 0:
                    sp.wait_ge(s["xhat2"], g - 2)
                    sp.dma_start(hn2_d[:, g - 3, :], hn[:, 1, (g - 3) % 2, :]).then_inc(hn2_stored[(g - 3) % 2], 16)
                for n in range(3):
                    refill(g, n)
                place(g, 0)
                if 0 <= g - 2 < G:
                    sp.wait_ge(s["x1_ready"], g - 1)
                    sp.dma_start(x1_d[:, g - 2, :], x1[:, g % 2, :]).then_inc(x1_stored[g % 2], 16)
                place(g, 1)
                refill(g, 3)
                for n in range(2, NPLACES):
                    place(g, n)
                refill(g, 4)
            left = list(LEFT)
            while left[0] < TAIL:
                slot(left.pop(0))
            for step in GROUPS[NG - 1]:
                if step + 2 < G:
                    rows_back(step + 2)
                if left[0] + 3 < FIRST[NG - 1]:
                    slot(left.pop(0))

            def combine_in(g):
                c, p = half_of(g)
                i = g % NC
                if g >= NC:
                    sp.wait_ge(s["out_ready"], g - NC + 1)
                sp.dma_start(x1buf[:, i, :], x1_d[:, g, :]).then_inc(base_in[i], 16)
                sp.dma_start(xbuf[:, i, :], x[p, c * P:(c + 1) * P, :]).then_inc(base_in[i], 16)

            def combine_out(g):
                c, p = half_of(g)
                sp.wait_ge(s["out_ready"], g + 1)
                sp.dma_start(out[p, c * P:(c + 1) * P, :], obuf[:, g % NC, :]).then_inc(stored[g % NC], 16)

            for i in range(2):
                sp.wait_ge(x1_stored[i], 16 * (G // 2))
            while left[0] < COMBINE:
                slot(left.pop(0))
            sp.wait_ge(s["pv_piece"], PIECES[G])
            for g in range(NC):
                combine_in(g)
            for g in range(G):
                while left and left[0] <= slots_before(g):
                    slot(left.pop(0))
                if g + NC < G:
                    combine_in(g + NC)
                combine_out(g)
            for i in range(NC):
                sp.wait_ge(stored[i], 16 * (G // NC))

        @block.gpsimd
        def _(pool):
            links = [0]

            def link(ins):
                links[0] += 1
                ins.then_inc(s["pool_chain"], 1)
                pool.wait_ge(s["pool_chain"], links[0])

            link(pool.memset(rstd[:, 2:3], -0.5))
            link(pool.memset(ident[:, :], 0.0))
            pool.affine_select(out=ident[:, :], in_=ident[:, :], compare_op=ALU.not_equal, fill=1.0, base=0,
                               pattern=[[-1, P]], channel_multiplier=1).then_inc(s["const_ready"], 1)
            pool.wait_ge(s["z_in"], 16 * 3)
            link(pool.tensor_tensor(alpha[:, 0, :], z[:, 0, :], z[:, 1, :], ALU.add))
            link(pool.tensor_scalar(alpha[:, 0, :], alpha[:, 0, :], -2.0, None, ALU.mult))
            link(pool.tensor_tensor(alpha[:, 0, :], alpha[:, 0, :], z[:, 2, :], ALU.add))
            pool.tensor_scalar(alpha[:, 1, :], z[:, 2, :], -1.0, None, ALU.mult).then_inc(s["alpha_ready"], 1)

            def later_constants():
                link(pool.memset(ones_b[:, :], 1.0))
                pool.affine_select(out=lower[:, :], in_=ones_b[:, :], compare_op=ALU.is_gt, fill=0.0, base=0,
                                   pattern=[[1, P]], channel_multiplier=-1).then_inc(s["const_ready"], 1)
                pool.memset(ones_r[:, :].bitcast(F32), 1.0).then_inc(s["const_ready"], 1)
                pool.memset(zeros[:, :], 0.0).then_inc(s["zero_ready"], 1)
                link(pool.iota(iota_i[:, :], [[1, max(NTILES)]], base=0, channel_multiplier=0))
                pool.tensor_copy(iota_t[:, :], iota_i[:, :]).then_inc(s["const_ready"], 1)

            def w1_low(e):
                if e == E - 1:
                    pool.wait_ge(s["bias_lo_in"], 16)
                pool.wait_ge(s["w1_hi_ready"], e + 1)
                part = slice(e * HC * F, (e + 1) * HC * F)
                pool.tensor_tensor(w1_lo[:, part], w1raw[e % 2],
                                   w1_hi[:, part].bitcast(F32), ALU.subtract).then_inc(s["w1_lo_ready"], 1)

            def neighbours(g):
                i = g % 2
                pool.wait_ge(x_in[i], 64 * (g // 2 + 1))
                link(pool.tensor_copy(xp[:, i, 0:H + 2:H + 1], xp[:, i, 2:H:H - 3]))
                link(pool.tensor_tensor(xud[:, i, 0, :], xud[:, i, 0, :], xud[:, i, 1, :], ALU.add))
                pool.tensor_tensor(xud[:, i, 1, :], xp[:, i, 0:H], xp[:, i, 2:H + 2], ALU.add).then_inc(s["sums_ready"], 1)

            def diffuse(g):
                i = g % 2
                d = du[:, g % DU, :]
                pool.wait_ge(s["scaled"], 3 * (g + 1))
                link(pool.tensor_tensor(d, d, xp[:, i, 1:H + 1], ALU.mult))
                link(pool.tensor_tensor(d, d, xud[:, i, 0, :], ALU.add))
                pool.tensor_tensor(d, d, xud[:, i, 1, :], ALU.add).then_inc(s["du_ready"], 1)

            def deviation(g, k):
                pool.wait_ge(s[("stats1", "stats2")[k]], g + 1)
                link(pool.tensor_scalar(rstd[:, k:k + 1], mv[:, k, 1:2], EPS, None, ALU.add))
                pool.tensor_tensor(rstd[:, k:k + 1], rstd[:, k:k + 1], rstd[:, 2:3], ALU.pow).then_inc(s[("rstd1", "rstd2")[k]], 1)

            def scatter(g):
                for r in range(NG):
                    if g == GROUPS[r][0]:
                        pool.wait_ge(s["slots_ready"], r + 1)
                        pool.wait_ge(zero_done[r], 16 * len([t for t in ZEROS if t[2] == r]))
                pool.wait_ge(rows_in[g % 2], 16 * (g // 2 + 1))
                for k in range(2):
                    pool.indirect_dma_start(xs_d, bass.IndirectOffsetOnAxis(ap=slot_row[:, k, g:g + 1], axis=0),
                                            rows[:, g % 2, :], None).then_inc(scattered[g % 2], 16)

            def gather(g):
                i = g % NC
                if g >= NC:
                    pool.wait_ge(s["out_ready"], g - NC + 1)
                for k in range(2):
                    pool.indirect_dma_start(gbuf[:, i, k, :], None, ys_d[0:FIRST[[r for r in range(NG) if g in GROUPS[r]][0] + 1] * P, :],
                                            bass.IndirectOffsetOnAxis(ap=slot_row[:, k, g:g + 1], axis=0)).then_inc(gathered[i], 16)

            def low(j):
                pool.wait_ge(s["xT_hi_sb"], j + 1)
                pool.tensor_tensor(xT_lo[:, :, :].rearrange("p k b -> p (k b)"), xT[:, :],
                                   xT_hi[:, :, :].rearrange("p k b -> p (k b)").bitcast(F32), ALU.subtract).then_inc(s["xT_lo_sb"], 1)

            def slot(j):
                if j == -1:
                    low(0)
                if j + 2 < ALL:
                    low(j + 2)

            def place(g, n):
                for j in SLOTS[g, n]:
                    slot(j)

            def scatter_at(g, n):
                if (g, n) in SCATTER:
                    scatter(SCATTER[g, n])

            for g in range(-3, G + 3):
                if 0 <= g + 2 < G:
                    deviation(g + 2, 0)
                scatter_at(g, 0)
                if g + 3 < G:
                    neighbours(g + 3)
                scatter_at(g, 1)
                if 0 <= g - 2 < G:
                    deviation(g - 2, 1)
                if g + 3 < G and not diffused_late(g):
                    diffuse(g + 3)
                if g == -3:
                    later_constants()
                scatter_at(g, 2)
                place(g, 0)
                place(g, 1)
                if g + 3 < G and diffused_late(g):
                    diffuse(g + 3)
                scatter_at(g, 3)
                place(g, 2)
                if 0 <= g - W1_FROM < E:
                    w1_low(g - W1_FROM)
                for n in range(3, NPLACES):
                    place(g, n)
                scatter_at(g, 4)
            for j in LEFT:
                if j < TAIL:
                    slot(j)
            for g in GROUPS[NG - 1]:
                scatter(g)
            pool.wait_ge(s["pv_piece"], PIECES[G])
            for g in range(G):
                if g in (GROUPS[0][0], GROUPS[NG - 1][0]):
                    n = FIRST[NG - 1] if g == 0 else ALL
                    pool.wait_ge(y_out[0], 16 * ((n + 1) // 2))
                    pool.wait_ge(y_out[1], 16 * (n // 2))
                gather(g)

        @block.scalar
        def _(act):
            def flat(t):
                return t[:, :, :].rearrange("p k b -> p (k b)")

            def scale(g):
                i, p = g % 2, g % S
                if g == 0:
                    act.wait_ge(s["alpha_ready"], 1)
                if g >= DU:
                    act.wait_ge(s["x1_ready"], g - DU + 1)
                act.wait_ge(x_in[i], 64 * (g // 2 + 1))
                act.activation(du[:, g % DU, :], xp[:, i, 1:H + 1], ACT.Identity, bias=alpha[:, 0, p:p + 1],
                               scale=alpha[:, 1, p:p + 1]).then_inc(s["scaled"], 1)
                act.wait_ge(s["sums_ready"], g + 1)
                act.activation(xud[:, i, 0, :], xud[:, i, 0, :], ACT.Copy, scale=z[:, 1, p:p + 1]).then_inc(s["scaled"], 1)
                act.activation(xud[:, i, 1, :], xud[:, i, 1, :], ACT.Copy, scale=z[:, 0, p:p + 1]).then_inc(s["scaled"], 1)

            def affine(dst, bank, k):
                for c in range(HC):
                    ins = act.activation(dst[:, c * P:(c + 1) * P], bank[:, c * P:(c + 1) * P], ACT.Identity,
                                         scale=ln[:, 2 * k, c:c + 1], bias=ln[:, 2 * k + 1, c:c + 1])
                return ins

            def setup():
                act.wait_ge(s["bias_in"], 32)
                act.activation(bias[0:1, :], braw.rearrange("o a h -> o (a h)"), ACT.Copy).then_inc(s["bias_split"], 1)
                for k in range(HC):
                    qk_bank, vo_bank = ((b_x, b_h), (b_t, b_y))[k]
                    act.wait_ge(s["wT_ready"], 2 * k + 1)
                    act.activation(wqkv[:, k, 0:2 * H], qk_bank[:, :], ACT.Copy).then_inc(s["wT_sb"], 1)
                    act.wait_ge(s["wT_ready"], 2 * k + 2)
                    act.activation(wqkv[:, k, 2 * H:3 * H], vo_bank[:, 0:H], ACT.Copy).then_inc(s["wT_sb"], 1)
                    act.activation(wo[:, k, :], vo_bank[:, H:2 * H], ACT.Copy).then_inc(s["wT_sb"], 1)
                act.wait_ge(s["wT_ready"], 5)
                act.activation(wr[:, :], b_at[:, 0:HC * E], ACT.Copy).then_inc(s["wr_sb"], 1)

            def w1_high(e):
                act.wait_ge(w1_staged[e % 2], 16 * (e // 2 + 1))
                part = slice(e * HC * F, (e + 1) * HC * F)
                act.activation(w1_hi[:, part], w1raw[e % 2],
                               ACT.Copy).then_inc(s["w1_hi_ready"], 1)

            def turned_in(j):
                act.wait_ge(s["x_tr"], j + 1)
                affine(xT, b_x, 1).then_inc(s["xT_sb"], 1)
                act.wait_ge(s["xT_sb"], j + 1)
                act.activation(flat(xT_hi), xT[:, :], ACT.Copy).then_inc(s["xT_hi_sb"], 1)

            def gelu(j):
                act.wait_ge(s["h_ready"], j + 1)
                act.activation(hm[:, :], b_h[:, :], ACT.Gelu).then_inc(s["gelu_done"], 1)

            def turned_h(j):
                act.wait_ge(s["hT2_ready"], j + 1)
                act.activation(hmT[:, :], b_t[:, :], ACT.Copy).then_inc(s["hmT_sb"], 1)

            def result(j):
                act.wait_ge(s["y_ready"], j + 1)
                if j >= 2:
                    act.wait_ge(y_out[j % 2], 16 * (j // 2))
                act.activation(y[:, j % 2, :], b_y[:, 0:H], ACT.Copy).then_inc(s["y_sb"], 1)

            def slot(j):
                if j == -1:
                    turned_in(0)
                else:
                    turned_h(j)
                if 0 <= j - 1 < TAIL:
                    result(j - 1)
                if j + 1 < ALL:
                    gelu(j + 1)
                if j + 2 < ALL:
                    turned_in(j + 2)

            def place(g, n):
                for j in SLOTS[g, n]:
                    slot(j)

            def exponentials(g):
                n = NH * (g % S + 1)
                act.wait_ge(s["sc_ready"], g + 1)
                act.activation(pr[:, g % 2, 0:n], sc[:, g % 2, 0:n], ACT.Exp, scale=SCALE).then_inc(s["exp_ready"], 1)

            def queries_keys(g):
                p = g % S
                act.wait_ge(s["qkv_ready"], g + 1)
                act.activation(q[:, g % 2, :], b_qk[:, 0:H], ACT.Copy).then_inc(s["qk_sb"], 1)
                if p == 0 and g > 0:
                    act.wait_ge(s["sc_ready"], g)
                act.activation(kv[:, p, :], b_qk[:, H:2 * H], ACT.Copy).then_inc(s["qk_sb"], 1)

            def values(g):
                if g == S:
                    act.wait_ge(s["pv_piece"], PIECES[S - 1] + 1)
                act.activation(kv[:, S + g % S, :], b_v[:, 0:H], ACT.Copy).then_inc(s["v_sb"], 1)

            def odds(r):
                n = len(GROUPS[r])
                act.wait_ge(s["rt_sub"], r + 1)
                act.activation(rt(1, n)[:, 0:2 * n], rt(1, n)[:, 0:2 * n], ACT.Exp)
                act.activation(rt(0, n), rt(0, n), ACT.Exp).then_inc(s["rt_exp"], 1)

            act.wait_ge(s["alpha_ready"], 1)
            act.activation(junk[:, 1:2], alpha[:, 0, 0:1], ACT.Copy)
            for g in range(-3, G + 3):
                if 0 <= g - 2 < G:
                    act.wait_ge(s["pv_used"], PIECES[g - 1])
                    if g - 2 >= 1:
                        act.wait_ge(s["o_ready"], g - 2)
                    act.activation(flat(aT), b_at[:, 0:H], ACT.Copy).then_inc(s["aT_sb"], 1)
                if g - 3 >= 0:
                    act.wait_ge(s["h2T_ready"], g - 2)
                    if g - 3 >= 1:
                        act.wait_ge(s["lg_ready"], g - 3)
                    affine(flat(h2T), b_tr, 1).then_inc(s["h2T_sb"], 1)
                if g == -3:
                    scale(0)
                    setup()
                if 0 <= g - 1 < G:
                    exponentials(g - 1)
                if 0 < g + 3 < G and not diffused_late(g):
                    scale(g + 3)
                if g >= 0 and SLOTS[g, 0] and g < G:
                    act.activation(junk[:, 0:1], junk[:, 1:2], ACT.Gelu)
                if g == S:
                    values(S)
                if 0 <= g + 1 < G:
                    queries_keys(g + 1)
                    if g + 1 != S:
                        values(g + 1)
                if 0 <= g - W1_FROM < E:
                    w1_high(g - W1_FROM)
                place(g, 0)
                if 0 <= g + 2 < G:
                    act.wait_ge(s["hT_ready"], g + 3)
                    if g == -2:
                        act.wait_ge(s["params_in"], 16 * 4)
                    if g + 2 >= 1:
                        act.wait_ge(s["qkv_ready"], g + 2)
                    affine(flat(hT), b_tr, 0).then_inc(s["hT_sb"], 1)
                place(g, 1)
                if 0 < g + 3 < G and diffused_late(g):
                    scale(g + 3)
                if g - 3 >= 0:
                    act.wait_ge(s["lg_ready"], g - 2)
                    act.activation(logits[:, g - 3, :], b_tr[:, H:H + E], ACT.Copy).then_inc(s["lg_sb"], 1)
                for n in range(2, NPLACES):
                    place(g, n)
                if g in ROUTE:
                    odds(ROUTE[g])
            for j in LEFT[:1]:
                slot(j)
            odds(NG - 1)
            for j in range(LEFT[1], TAIL + 2):
                slot(j)
            with act.Fori(0, LOOPS) as n:
                for i in range(2):
                    j = n * 2 + (TAIL + 2 + i)
                    turned_h(j)
                    gelu(j + 1)
                    turned_in(j + 2)
            for j in range(TAIL + 2 + 2 * LOOPS, ALL):
                slot(j)

        @block.vector
        def _(dve):
            count = [0]

            def tick(ins):
                count[0] += 1
                ins.then_inc(s["dve_chain"], 1)
                return count[0]

            def need(n):
                dve.wait_ge(s["dve_chain"], n)

            def link(ins):
                need(tick(ins))

            def spread(col, n, m):
                return col.rearrange("p (n o) -> p n o", o=1).to_broadcast([P, n, m])

            dve.wait_ge(s["bias_split"], 1)
            dve.tensor_tensor(blo, braw.rearrange("o a h -> o (a h)"), bias[0:1, :].bitcast(F32),
                              ALU.subtract).then_inc(s["bias_split"], 1)

            def unit(src, g, k):
                dve.wait_ge(s[("rstd1", "rstd2")[k]], g + 1)
                if g >= 2:
                    dve.wait_ge(s[("hT_ready", "h2T_ready")[k]], g - 1)
                    if k == 1:
                        dve.wait_ge(hn2_stored[g % 2], 16 * (g // 2))
                dve.tensor_scalar(hn[:, k, g % 2, :], src, mv[:, k, 0:1], rstd[:, k:k + 1], ALU.subtract,
                                  ALU.mult).then_inc(s[("xhat1", "xhat2")[k]], 1)

            def low(j):
                dve.wait_ge(s["xT_hi_sb"], j + 1)
                dve.tensor_tensor(xT_lo[:, :, :].rearrange("p k b -> p (k b)"), xT[:, :],
                                  xT_hi[:, :, :].rearrange("p k b -> p (k b)").bitcast(F32), ALU.subtract).then_inc(s["xT_lo_sb"], 1)

            def result(j):
                dve.wait_ge(s["y_ready"], j + 1)
                dve.wait_ge(y_out[j % 2], 16 * (j // 2))
                dve.tensor_copy(y[:, j % 2, :], b_y[:, 0:H]).then_inc(s["y_sb"], 1)

            def slot(j):
                if j + 2 < ALL:
                    low(j + 2)
                result(j)

            def top(g):
                dve.wait_ge(s["lg_sb"], g + 1)
                n = tick(dve.max(top8[:, g, :], logits[:, g, :]))
                return n, g

            def top_index(n_g):
                n, g = n_g
                need(n)
                return tick(dve.max_index(idx8[:, g, :], top8[:, g, :], logits[:, g, :]))

            def route(r, last):
                g0, n = GROUPS[r][0], len(GROUPS[r])
                g1 = g0 + n
                oh = rt(0, n, 2).rearrange("p (k g e) -> p k g e", k=2, e=E)
                both = rt(2, n, 2)
                cum, tot, Cv, Dv = [x.rearrange("p (g e) -> p g e", e=E) for x in
                                    (both[:, 0:n * E], both[:, n * E:2 * n * E], rt(4, n), rt(5, n))]
                need(last)
                link(dve.tensor_copy(idxf[:, :, 0:n].rearrange("p k g -> p g k"), idx8[:, g0:g1, 0:2]))
                io = iota_t[:, 0:E].rearrange("p (o e) -> p o e", o=1).to_broadcast([P, n, E])
                for k in range(2):
                    last = dve.tensor_tensor(oh[:, k], io, idxf[:, k, 0:n].rearrange("p (g o) -> p g o", o=1).to_broadcast([P, n, E]),
                                             ALU.is_equal)
                link(last)
                dve.tensor_tensor(chosen[:, 0:n * E].rearrange("p (g e) -> p g e", e=E), oh[:, 0], oh[:, 1],
                                  ALU.add).then_inc(s["rt_m"], 1)
                dve.wait_ge(s["rt_cum"], r + 1)
                dve.tensor_copy(both, b_tr[:, 0:2 * n * E]).then_inc(s["rt_cum_sb"], 1)
                dve.wait_ge(s["rt_cum_sb"], r + 1)
                src, dst, step = tot, Cv, 1
                while step < n:
                    dve.tensor_copy(dst[:, 0:step, :], src[:, 0:step, :])
                    link(dve.tensor_tensor(dst[:, step:n, :], src[:, step:n, :], src[:, 0:n - step, :], ALU.add))
                    src, dst, step = dst, (Dv if dst is Cv else Cv), 2 * step
                ones, nt, endt, first = [small[:, 8 * i:8 * i + 8] for i in range(4)]
                nti = smalli[:, 0:8]
                link(dve.tensor_scalar(nti, src[:, n - 1, :], float(P - 1), None, ALU.add))
                dve.memset(ones, 1.0)
                last = tick(dve.tensor_scalar(nti, nti, 7, None, ALU.arith_shift_right))
                link(dve.tensor_tensor(dst, src, tot, ALU.subtract))
                dve.tensor_copy(nt, nti)
                link(dve.tensor_tensor(dst, dst, cum, ALU.add))
                link(dve.tensor_tensor_scan(endt, ones, nt, 0.0, ALU.mult, ALU.add))
                tiles = NTILES[r]
                tt = qk_prod[:, 1, 0:tiles * E].rearrange("p (t e) -> p t e", e=E)
                te = qk_prod[:, 1, tiles * E:tiles * (E + 1)]
                last = tick(dve.tensor_tensor(first, endt, nt, ALU.subtract))
                made = tick(dve.tensor_tensor(tt, spread(iota_t[:, 0:tiles], tiles, E),
                                              endt.rearrange("p (o e) -> p o e", o=1).to_broadcast([P, tiles, E]), ALU.is_ge))
                need(last)
                last = tick(dve.tensor_scalar(first, first, float(P), float(FIRST[r] * P), ALU.mult, ALU.add))
                need(made)
                made = tick(dve.tensor_reduce(te, tt, AX, ALU.add))
                need(last)
                last = tick(dve.tensor_tensor(dst, dst, first.rearrange("p (o e) -> p o e", o=1).to_broadcast([P, n, E]), ALU.add))
                need(made)
                made = tick(dve.tensor_scalar(te, te, float(E - 1), None, ALU.min))
                need(last)
                for k in range(2):
                    last = tick(dve.tensor_tensor(oh[:, k], oh[:, k], dst, ALU.mult))
                need(made)
                dve.tensor_copy(tab[:, FIRST[r]:FIRST[r + 1]], te)
                need(last)
                link(dve.tensor_reduce(idxf[:, :, 0:n], oh, AX, ALU.add))
                dve.tensor_copy(slot_row[:, :, g0:g1], idxf[:, :, 0:n]).then_inc(s["slots_ready"], 1)
                lg, most = logits[:, g0:g1, :], top8[:, g0:g1, 0:1]
                A = rt(0, n).rearrange("p (g e) -> p g e", e=E)
                g2 = rt(1, n)[:, 0:2 * n].rearrange("p (g k) -> p g k", k=2)
                col = rt(5, n)[:, 0:n]
                dve.wait_ge(s["slots_ready"], r + 1)
                dve.tensor_tensor(g2, top8[:, g0:g1, 0:2], most.to_broadcast([P, n, 2]), ALU.subtract)
                dve.tensor_tensor(A, lg, most.to_broadcast([P, n, E]), ALU.subtract).then_inc(s["rt_sub"], 1)
                dve.wait_ge(s["rt_exp"], r + 1)
                link(dve.tensor_reduce(col, A, AX, ALU.add))
                link(dve.reciprocal(col, col))
                link(dve.tensor_tensor(gates[:, g0:g1, :], g2, spread(col, n, 2), ALU.mult))

            for g in range(-3, G + 3):
                T = g % S + 1
                aggregated = False

                def stats():
                    dve.wait_ge(s["du_ready"], g + 3)
                    return tick(dve.bn_stats(small[:, 48:54], du[:, (g + 2) % DU, :]))

                def aggregate(st):
                    need(st)
                    if g + 2 >= 1:
                        dve.wait_ge(s["xhat1"], g + 2)
                    dve.bn_aggr(mv[:, 0, :], small[:, 48:54]).then_inc(s["stats1"], 1)

                if 0 <= g < G:
                    scv = sc[:, g % 2, 0:NH * T].rearrange("p (n t) -> p n t", t=T)
                    dve.wait_ge(s["qk_sb"], 2 * (g + 1))
                    if g >= 2:
                        dve.wait_ge(s["exp_ready"], g - 1)
                    made, summed = [], []

                    def multiply(m):
                        t0, t1 = m * TP, min(T, m * TP + TP)
                        if m >= 2:
                            need(summed[m - 2])
                        made.append(tick(dve.tensor_tensor(
                            qk_prod[:, m % 2, 0:(t1 - t0) * H].rearrange("p (t h) -> p t h", h=H),
                            q[:, g % 2, :].rearrange("p (o h) -> p o h", o=1).to_broadcast([P, t1 - t0, H]),
                            kv[:, t0:t1, :], ALU.mult)))

                    def add_up(m):
                        t0, t1 = m * TP, min(T, m * TP + TP)
                        need(made[m])
                        summed.append(tick(dve.tensor_reduce(
                            scv.rearrange("p n t -> p t n")[:, t0:t1, :],
                            qk_prod[:, m % 2, 0:(t1 - t0) * H].rearrange("p (t n d) -> p t n d", n=NH, d=D), AX, ALU.add)))

                    for m in range(NPIECE[g]):
                        multiply(m)
                        if m == 0 and g + 2 < G:
                            st = stats()
                        if m >= 1:
                            add_up(m - 1)
                        if m == 1 and g + 2 < G:
                            aggregate(st)
                            aggregated = True
                    add_up(NPIECE[g] - 1)
                if 0 <= g + 2 < G and not aggregated:
                    aggregate(st if g >= 0 else stats())
                if 0 <= g < G:
                    need(summed[-1])
                    link(dve.tensor_reduce(small[:, 0:NH], scv, AX, ALU.max))
                    dve.tensor_tensor(scv, scv, spread(small[:, 0:NH], NH, T), ALU.subtract).then_inc(s["sc_ready"], 1)
                if 0 <= g - 2 < G:
                    dve.wait_ge(s["o_ready"], g - 1)
                    if g - 2 >= 2:
                        dve.wait_ge(x1_stored[g % 2], 16 * ((g - 2) // 2))
                    dve.tensor_tensor(x1[:, g % 2, :], du[:, (g - 2) % DU, :], b_at[:, H:2 * H], ALU.add).then_inc(s["x1_ready"], 1)
                if 0 <= g + 2 < G:
                    unit(du[:, (g + 2) % DU, :], g + 2, 0)
                st = None
                if 0 <= g - 2 < G:
                    dve.wait_ge(s["x1_ready"], g - 1)
                    st = tick(dve.bn_stats(small[:, 54:60], x1[:, g % 2, :]))

                v = g - 1
                T = v % S + 1
                if 0 <= v < G:
                    dve.wait_ge(s["exp_ready"], v + 1)
                    prv = pr[:, v % 2, 0:NH * T].rearrange("p (n t) -> p n t", t=T)
                    total = tick(dve.tensor_reduce(small[:, 16:16 + NH], prv, AX, ALU.add))
                    if st:
                        need(st)
                        if g - 2 >= 1:
                            dve.wait_ge(s["xhat2"], g - 2)
                        dve.bn_aggr(mv[:, 1, :], small[:, 54:60]).then_inc(s["stats2"], 1)
                        st = None
                    need(total)
                    total = tick(dve.reciprocal(small[:, 32:32 + NH], small[:, 16:16 + NH]))
                    ordered = top(g - 4) if 0 <= g - 4 and g - 1 not in ROUTE else None
                    need(total)
                    total = tick(dve.tensor_tensor(prv, prv, spread(small[:, 32:32 + NH], NH, T), ALU.mult))
                    if ordered:
                        top_index(ordered)
                    need(total)
                    dve.wait_ge(s["v_sb"], v + 1)

                    def value_products(m):
                        t0, t1 = m * TP, min(T, m * TP + TP)
                        at = PIECES[v] + m
                        if at >= NPV:
                            dve.wait_ge(s["pv_used"], at - NPV + 1)
                        ins = dve.tensor_tensor(pv_prod[:, at % NPV, 0:(t1 - t0) * H].rearrange("p (t n d) -> p t n d", n=NH, d=D),
                                                kv[:, S + t0:S + t1, :].rearrange("p t (n d) -> p t n d", d=D),
                                                pr[:, v % 2, 0:NH * T].rearrange("p (n t o) -> p t n o", t=T, o=1)[:, t0:t1, :, :].to_broadcast([P, t1 - t0, NH, D]),
                                                ALU.mult)
                        n = t1 - t0
                        if rows_left(v, n) == n:
                            ins.then_inc(s["pv_piece"], 1)
                        else:
                            open_pieces.append((m, n, tick(ins)))

                    def fold():
                        for i in range(len(open_pieces)):
                            m, n, done = open_pieces.pop(0)
                            keep = n - n // 2
                            pv = pv_prod[:, (PIECES[v] + m) % NPV, :]
                            need(done)
                            ins = dve.tensor_tensor(pv[:, 0:(n - keep) * H], pv[:, 0:(n - keep) * H], pv[:, keep * H:n * H], ALU.add)
                            if keep == rows_left(v, min(TP, T - m * TP)):
                                ins.then_inc(s["pv_piece"], 1)
                            else:
                                open_pieces.append((m, keep, tick(ins)))

                    open_pieces = []
                    for m in range(NPIECE[v]):
                        if T - m * TP == 1:
                            while open_pieces:
                                fold()
                        before, open_pieces = open_pieces, []
                        value_products(m)
                        this, open_pieces = open_pieces, before
                        fold()
                        open_pieces += this
                    while open_pieces:
                        fold()
                if st:
                    need(st)
                    dve.wait_ge(s["xhat2"], g - 2)
                    dve.bn_aggr(mv[:, 1, :], small[:, 54:60]).then_inc(s["stats2"], 1)
                if 0 <= g - 2 < G:
                    unit(x1[:, g % 2, :], g - 2, 1)
                for step in ([g - 4, g - 3] if g == G + 1 else [g - 3] if g in ROUTE or g > G + 1 else []):
                    last = top_index(top(step))
                if g in ROUTE:
                    if ROUTE[g] == 0:
                        dve.wait_ge(s["const_ready"], 4)
                    route(ROUTE[g], last)
            route(NG - 1, last)

            def combine(g):
                i = g % NC
                dve.wait_ge(base_in[i], 32 * (g // NC + 1))
                link(dve.tensor_tensor(x1buf[:, i, :], x1buf[:, i, :], xbuf[:, i, :], ALU.add))
                dve.wait_ge(gathered[i], 32 * (g // NC + 1))
                link(dve.scalar_tensor_tensor(out=x1buf[:, i, :], in0=gbuf[:, i, 0, :], scalar=gates[:, g, 0:1],
                                              in1=x1buf[:, i, :], op0=ALU.mult, op1=ALU.add))
                if g >= NC:
                    dve.wait_ge(stored[i], 16 * (g // NC))
                dve.scalar_tensor_tensor(out=obuf[:, i, :], in0=gbuf[:, i, 1, :], scalar=gates[:, g, 1:2],
                                         in1=x1buf[:, i, :], op0=ALU.mult, op1=ALU.add).then_inc(s["out_ready"], 1)

            left = list(range(TAIL, ALL))
            while left[0] < COMBINE:
                slot(left.pop(0))
            for g in range(G):
                while left and left[0] < slots_before(g):
                    slot(left.pop(0))
                combine(g)

        @block.tensor
        def _(pe):
            pe.wait_ge(s["const_ready"], 1)
            pe.wait_ge(s["win_in"], 16 * 3)
            for k in range(HC):
                for bank, t0 in (((b_x, b_h), (b_t, b_y))[k][0], 0), (((b_x, b_h), (b_t, b_y))[k][1], 4):
                    for t in range(4):
                        mm = pe.transpose(bank[:, t * P:(t + 1) * P], wraw[:, t0 + t, k * P:(k + 1) * P], ident[:, :])
                    mm.then_inc(s["wT_ready"], 1)
            for k in range(HC):
                mm = pe.transpose(b_at[:, k * E:(k + 1) * E], wrraw[:, k * P:(k + 1) * P], ident[0:E, 0:E])
            mm.then_inc(s["wT_ready"], 1)

            def turn_in(j, i, loads):
                pe.wait_ge(xin_in[i], loads * 16)
                if not (isinstance(j, int) and j == 0):
                    pe.wait_ge(s["xT_sb"], j)
                for k in range(HC):
                    mm = pe.transpose(b_x[:, k * P:(k + 1) * P], xin[:, i, k * P:(k + 1) * P], ident[:, :])
                mm.then_inc(s["x_tr"], 1)

            def expert(j):
                return pe.value_load(tab[0:1, bass.ds(j, 1)], min_val=0, max_val=E - 1)

            def up(j, e):
                pe.wait_ge(s["xT_lo_sb"], j + 1)
                for k in range(HC):
                    cols = bass.ds(e * (HC * F) + k * F, F)
                    pe.matmul(b_h[:, :], xT_hi[:, k, :], w1_hi[:, cols], start=(k == 0), stop=False)
                    pe.matmul(b_h[:, :], xT_hi[:, k, :], w1_lo[:, cols], start=False, stop=False)
                    mm = pe.matmul(b_h[:, :], xT_lo[:, k, :], w1_hi[:, cols], start=False, stop=(k == HC - 1))
                mm.then_inc(s["h_ready"], 1)

            def turn_h(j):
                pe.wait_ge(s["gelu_done"], j + 1)
                for k in range(FC):
                    mm = pe.transpose(b_t[:, k * P:(k + 1) * P], hm[:, k * P:(k + 1) * P], ident[:, :])
                mm.then_inc(s["hT2_ready"], 1)

            def down(j, e):
                pe.wait_ge(s["hmT_sb"], j + 1)
                if not (isinstance(j, int) and j == 0):
                    pe.wait_ge(s["y_sb"], j)
                for k in range(FC):
                    mm = pe.matmul(b_y[:, 0:H], hmT[:, k * P:(k + 1) * P], w2_s[:, bass.ds(e * (FC * H) + k * H, H)],
                                   start=(k == 0), stop=(k == FC - 1))
                mm.then_inc(s["y_ready"], 1)

            def next_expert(j):
                if j in FIRST:
                    pe.wait_ge(s["slots_ready"], group_of(j) + 1)
                return expert(j)

            loaded = {}

            def slot(j):
                if j == -1:
                    pe.wait_ge(s["w1_lo_ready"], E)
                    pe.wait_ge(s["w2_in"], 16 * E)
                    turn_in(0, 0, 1)
                if j >= 0 and j not in loaded:
                    loaded[j] = expert(j)
                if j + 1 < ALL:
                    e_next = loaded[j + 1] = next_expert(j + 1)
                if j >= 0:
                    turn_h(j)
                if j + 1 < ALL:
                    up(j + 1, e_next)
                if j + 2 < ALL:
                    turn_in(j + 2, (j + 2) % 2, (j + 2) // 2 + 1)
                if j >= 0:
                    down(j, loaded.pop(j))

            def router(g):
                pe.wait_ge(s["h2T_sb"], g + 1)
                if g + 5 < G:
                    pe.wait_ge(s["hT_sb"], g + 6)
                for k in range(HC):
                    mm = pe.matmul(b_tr[:, H:H + E], h2T[:, k, :], wr[:, k * E:(k + 1) * E], start=(k == 0), stop=(k == HC - 1))
                mm.then_inc(s["lg_ready"], 1)

            def place(g, n):
                for j in SLOTS[g, n]:
                    slot(j)

            def count_tokens(r):
                n = len(GROUPS[r])
                pe.wait_ge(s["rt_m"], r + 1)
                pe.matmul(b_tr[:, 0:n * E], lower[:, :], chosen[:, 0:n * E], start=True, stop=True)
                pe.matmul(b_tr[:, n * E:2 * n * E], ones_b[:, :], chosen[:, 0:n * E], start=True, stop=True).then_inc(s["rt_cum"], 1)
                pe.wait_ge(s["rt_cum_sb"], r + 1)

            def project(g):
                pe.wait_ge(s["aT_sb"], g + 1)
                pe.matmul(b_at[:, H:2 * H], ones_r[:, :], bias[:, 3 * H:4 * H], start=True, stop=False)
                for k in range(HC):
                    mm = pe.matmul(b_at[:, H:2 * H], aT[:, k, :], wo[:, k, :], start=False, stop=(k == HC - 1))
                mm.then_inc(s["o_ready"], 1)

            def queries_keys_values(g):
                if g == 0:
                    pe.wait_ge(s["const_ready"], 3)
                    pe.wait_ge(s["wT_sb"], 6)
                    pe.wait_ge(s["wr_sb"], 1)
                    pe.wait_ge(s["bias_lo_in"], 16)
                pe.wait_ge(s["hT_sb"], g + 1)
                if g >= 1:
                    pe.wait_ge(s["qk_sb"], 2 * g)
                    pe.wait_ge(s["v_sb"], g)
                for bank, a, b in ((b_qk, 0, 2 * H), (b_v, 2 * H, 3 * H)):
                    pe.matmul(bank[:, 0:b - a], ones_r[:, :], bias[:, a:b], start=True, stop=False)
                    for k in range(HC):
                        mm = pe.matmul(bank[:, 0:b - a], hT[:, k, :], wqkv[:, k, a:b], start=False, stop=(k == HC - 1))
                mm.then_inc(s["qkv_ready"], 1)

            for g in range(-2, G + 3):
                if g - 3 >= 0:
                    pe.wait_ge(s["xhat2"], g - 2)
                    if g - 3 >= 1:
                        pe.wait_ge(s["lg_sb"], g - 3)
                    else:
                        pe.wait_ge(s["hT_sb"], g + 2)
                    for k in range(HC):
                        mm = pe.transpose(b_tr[:, k * P:(k + 1) * P], hn[:, 1, (g - 3) % 2, k * P:(k + 1) * P], ident[:, :])
                    mm.then_inc(s["h2T_ready"], 1)
                if projected_late(g) and 0 <= g + 1 < G:
                    queries_keys_values(g + 1)
                if 0 <= g - 2 < G:
                    project(g - 2)
                if not projected_late(g) and 0 <= g + 1 < G:
                    queries_keys_values(g + 1)
                place(g, 0)
                if 0 <= g + 2 < G:
                    pe.wait_ge(s["xhat1"], g + 3)
                    if g - 3 >= 0:
                        pe.wait_ge(s["h2T_sb"], g - 2)
                    elif g + 2 >= 1:
                        pe.wait_ge(s["hT_sb"], g + 2)
                    for k in range(HC):
                        mm = pe.transpose(b_tr[:, k * P:(k + 1) * P], hn[:, 0, g % 2, k * P:(k + 1) * P], ident[:, :])
                    mm.then_inc(s["hT_ready"], 1)
                place(g, 1)
                v = g - 1
                if 0 <= v < G:
                    T = v % S + 1
                    if v >= 1:
                        pe.wait_ge(s["x1_ready"], v)
                    for m in range(NPIECE[v]):
                        at = PIECES[v] + m
                        n = rows_left(v, min(TP, T - m * TP))
                        pe.wait_ge(s["pv_piece"], at + 1)
                        for t in range(n):
                            for k in range(HC):
                                lo = t * H + k * P
                                mm = pe.matmul(b_at[:, k * P:(k + 1) * P], pv_prod[:, at % NPV, lo:lo + P], ident[:, :],
                                               start=(m == 0 and t == 0 and k == 0), stop=(m == NPIECE[v] - 1 and t == n - 1),
                                               skip_group_check=True)
                        mm.then_inc(s["pv_used"], 1)
                        if m == 0 and g - 3 >= 0:
                            router(g - 3)
                        place(g, 2 + m)
                elif g - 3 >= 0:
                    router(g - 3)
                if g in ROUTE:
                    count_tokens(ROUTE[g])
            slot(LEFT[0])
            count_tokens(NG - 1)
            for j in range(LEFT[1], TAIL + 2):
                slot(j)
            with pe.Fori(0, LOOPS) as n:
                e = expert(n * 2 + (TAIL + 2))
                for i in range(2):
                    j = n * 2 + (TAIL + 2 + i)
                    e_next = expert(j + 1)
                    turn_h(j)
                    up(j + 1, e_next)
                    turn_in(j + 2, (TAIL + i) % 2, n + ((TAIL + 4 + i) // 2 + 1))
                    down(j, e)
                    e = e_next
            loaded.clear()
            for j in range(TAIL + 2 + 2 * LOOPS, ALL):
                slot(j)


_INS = ["x", "condB_zX", "condB_zY", "condB_zR", "L0_ffn_ln1_w", "L0_ffn_ln1_b", "L0_ffn_in_proj_w",
        "L0_ffn_in_proj_b", "L0_ffn_out_proj_w", "L0_ffn_out_proj_b", "L0_ffn_ln2_w", "L0_ffn_ln2_b",
        "L0_ffn_router_w", "L0_ffn_w1", "L0_ffn_w2"]


def kernel(**inputs):
    import numpy as np
    import concourse.bacc as bacc
    from concourse.bass_utils import run_bass_kernel_spmd

    nc = bacc.Bacc("TRN2", target_bir_lowering=False, num_devices=1)
    arrays, args = {}, []
    for name in _INS:
        a = np.ascontiguousarray(inputs[name])
        arrays[f"in_{name}_dram"] = a
        args.append(nc.dram_tensor(f"in_{name}_dram", a.shape, mybir.dt.from_np(a.dtype), kind="ExternalInput").ap())
    out = nc.dram_tensor("out_dram", inputs["x"].shape, F32, kind="ExternalOutput").ap()
    adaln_moe_block(nc, *args, out)
    r = run_bass_kernel_spmd(nc, [arrays], core_ids=[0])
    return r.results[0]["out_dram"]
```
